# Optimizing a Trainium2 kernel written in Bass

```python
import numpy as np
import jax
import jax.numpy as jnp

def _softmax(x, axis=-1):
    return jax.nn.softmax(x, axis=axis)

def _gelu(x):
    return jax.nn.gelu(x, approximate=True)

def _silu(x):
    return jax.nn.silu(x)

def _sigmoid(x):
    return jax.nn.sigmoid(x)

def _layernorm(x, axis=-1, eps=1e-05):
    m = jnp.mean(x, axis=axis, keepdims=True)
    v = jnp.var(x, axis=axis, keepdims=True)
    return (x - m) / jnp.sqrt(v + eps)

def _scatter_add(tgt, idx, src, axis=0):
    return tgt.at[idx].add(src)

def _segment_sum(src, seg, n):
    return jax.ops.segment_sum(src, seg, n)
kernel_name = 'mk_sandwich_d1_jaxref_r8_a3af0e'

def setup_inputs(seed: int=0):
    np.random.seed(seed)
    _w = jnp.asarray

    def _L0_attn_setup():
        import jax, jax.numpy as jnp
        import numpy as np
        D_MODEL = 256
        N_HEADS = 16
        HEAD_DIM = D_MODEL // N_HEADS
        FF = 1024
        KCONV = 4
        EPS = 1e-05

        def _layernorm(x, w, b, eps=EPS):
            m = jnp.mean(x, axis=-1, keepdims=True)
            v = jnp.mean(jnp.square(x - m), axis=-1, keepdims=True)
            return (x - m) * jax.lax.rsqrt(v + eps) * w + b

        def _long_block(x, Wq, Wk, Wv, Wo, conv_w, conv_b, Wig, big, Wog, bog, Wg, bg, vnw, vnb, mnw, mnb, gnw, gnb, ln1w, ln1b, ln2w, ln2b, Wgate, Wval, Wout):
            B, T, C = x.shape
            H, D = (N_HEADS, HEAD_DIM)
            h = _layernorm(x, ln1w, ln1b)
            ht = jnp.transpose(h, (0, 2, 1))
            xc = jax.lax.conv_general_dilated(ht, conv_w, window_strides=(1,), padding=[(KCONV - 1, 0)], dimension_numbers=('NCH', 'OIH', 'NCH'), feature_group_count=C) + conv_b[None, :, None]
            x_conv = jax.nn.silu(jnp.transpose(xc, (0, 2, 1)))

            def l2norm(t):
                return t * jax.lax.rsqrt(jnp.sum(t * t, axis=-1, keepdims=True) + 1e-12)
            q = l2norm((h @ Wq).reshape(B, T, H, D))
            k = l2norm((h @ Wk).reshape(B, T, H, D))
            v = _layernorm((h @ Wv).reshape(B, T, H, D), vnw, vnb)
            i_gate = jax.nn.sigmoid(x_conv @ Wig + big).reshape(B, T, H, D)
            gamma = jax.nn.sigmoid(x_conv @ Wg + bg).reshape(B, T, H, 1)
            u = i_gate * k * v
            g = jnp.broadcast_to(gamma, u.shape)

            def combine(c1, c2):
                a1, b1 = c1
                a2, b2 = c2
                return (a1 * a2, a2 * b1 + b2)
            _, mem = jax.lax.associative_scan(combine, (g, u), axis=1)
            out = (_layernorm(mem, mnw, mnb) * q).reshape(B, T, C)
            og = out.reshape(B, T, H, D)
            m = jnp.mean(og, axis=-1, keepdims=True)
            var = jnp.mean(jnp.square(og - m), axis=-1, keepdims=True)
            og = (og - m) * jax.lax.rsqrt(var + EPS)
            out = (og * gnw.reshape(H, D) + gnb.reshape(H, D)).reshape(B, T, C)
            out = out * jax.nn.sigmoid(x_conv @ Wog + bog)
            h = x + out @ Wo
            h2 = _layernorm(h, ln2w, ln2b)
            mlp = jax.nn.silu(h2 @ Wgate) * (h2 @ Wval) @ Wout
            return h + mlp
        key = jax.random.key(seed)
        ks = jax.random.split(key, 32)
        B, T = (2, 512)
        s = lambda fan: 1.0 / np.sqrt(fan)
        inp = {'x': jax.random.normal(ks[0], (B, T, D_MODEL), jnp.float32), 'Wq': jax.random.normal(ks[1], (D_MODEL, D_MODEL), jnp.float32) * s(D_MODEL), 'Wk': jax.random.normal(ks[2], (D_MODEL, D_MODEL), jnp.float32) * s(D_MODEL), 'Wv': jax.random.normal(ks[3], (D_MODEL, D_MODEL), jnp.float32) * s(D_MODEL), 'Wo': jax.random.normal(ks[4], (D_MODEL, D_MODEL), jnp.float32) * s(D_MODEL), 'conv_w': jax.random.normal(ks[5], (D_MODEL, 1, KCONV), jnp.float32) * s(KCONV), 'conv_b': jnp.zeros((D_MODEL,), jnp.float32), 'Wig': jnp.zeros((D_MODEL, D_MODEL), jnp.float32), 'big': jnp.full((D_MODEL,), -3.0, jnp.float32), 'Wog': jax.random.normal(ks[6], (D_MODEL, D_MODEL), jnp.float32) * s(D_MODEL), 'bog': jnp.zeros((D_MODEL,), jnp.float32), 'Wg': jnp.zeros((D_MODEL, N_HEADS), jnp.float32), 'bg': jnp.asarray(np.log((lambda d: d / (1.0 - d))(1.0 - np.exp(np.linspace(np.log(1 - 0.9), np.log(1 - 0.999), N_HEADS)))), jnp.float32), 'vnw': jnp.ones((HEAD_DIM,), jnp.float32), 'vnb': jnp.zeros((HEAD_DIM,), jnp.float32), 'mnw': jnp.ones((HEAD_DIM,), jnp.float32), 'mnb': jnp.zeros((HEAD_DIM,), jnp.float32), 'gnw': jnp.ones((D_MODEL,), jnp.float32), 'gnb': jnp.zeros((D_MODEL,), jnp.float32), 'ln1w': jnp.ones((D_MODEL,), jnp.float32), 'ln1b': jnp.zeros((D_MODEL,), jnp.float32), 'ln2w': jnp.ones((D_MODEL,), jnp.float32), 'ln2b': jnp.zeros((D_MODEL,), jnp.float32), 'Wgate': jax.random.normal(ks[7], (D_MODEL, FF), jnp.float32) * s(D_MODEL), 'Wval': jax.random.normal(ks[8], (D_MODEL, FF), jnp.float32) * s(D_MODEL), 'Wout': jax.random.normal(ks[9], (FF, D_MODEL), jnp.float32) * s(FF)}
        return inp
    _L0_attn_in = _L0_attn_setup()

    def _L0_ffn_setup():
        import jax, jax.numpy as jnp
        import numpy as np
        E = 8
        TOP_K = 2
        H = 256
        I = 176
        SI = 704
        key = jax.random.key(seed)
        ks = jax.random.split(key, 9)
        s = lambda fan_in: 1.0 / np.sqrt(fan_in)
        return {'hidden_states': jax.random.normal(ks[0], (4, 256, H), dtype=jnp.float32), 'router_w': jax.random.normal(ks[1], (E, H), dtype=jnp.float32) * s(H), 'w_gate': jax.random.normal(ks[2], (E, H, I), dtype=jnp.float32) * s(H), 'w_up': jax.random.normal(ks[3], (E, H, I), dtype=jnp.float32) * s(H), 'w_down': jax.random.normal(ks[4], (E, I, H), dtype=jnp.float32) * s(I), 'sw_gate': jax.random.normal(ks[5], (H, SI), dtype=jnp.float32) * s(H), 'sw_up': jax.random.normal(ks[6], (H, SI), dtype=jnp.float32) * s(H), 'sw_down': jax.random.normal(ks[7], (SI, H), dtype=jnp.float32) * s(SI), 'shared_gate_w': jax.random.normal(ks[8], (H,), dtype=jnp.float32) * s(H)}
    _L0_ffn_in = _L0_ffn_setup()
    _d = {'L0_attn_x': _L0_attn_in['x'], 'L0_attn_Wq': _L0_attn_in['Wq'], 'L0_attn_Wk': _L0_attn_in['Wk'], 'L0_attn_Wv': _L0_attn_in['Wv'], 'L0_attn_Wo': _L0_attn_in['Wo'], 'L0_attn_conv_w': _L0_attn_in['conv_w'], 'L0_attn_conv_b': _L0_attn_in['conv_b'], 'L0_attn_Wig': _L0_attn_in['Wig'], 'L0_attn_big': _L0_attn_in['big'], 'L0_attn_Wog': _L0_attn_in['Wog'], 'L0_attn_bog': _L0_attn_in['bog'], 'L0_attn_Wg': _L0_attn_in['Wg'], 'L0_attn_bg': _L0_attn_in['bg'], 'L0_attn_vnw': _L0_attn_in['vnw'], 'L0_attn_vnb': _L0_attn_in['vnb'], 'L0_attn_mnw': _L0_attn_in['mnw'], 'L0_attn_mnb': _L0_attn_in['mnb'], 'L0_attn_gnw': _L0_attn_in['gnw'], 'L0_attn_gnb': _L0_attn_in['gnb'], 'L0_attn_ln1w': _L0_attn_in['ln1w'], 'L0_attn_ln1b': _L0_attn_in['ln1b'], 'L0_attn_ln2w': _L0_attn_in['ln2w'], 'L0_attn_ln2b': _L0_attn_in['ln2b'], 'L0_attn_Wgate': _L0_attn_in['Wgate'], 'L0_attn_Wval': _L0_attn_in['Wval'], 'L0_attn_Wout': _L0_attn_in['Wout'], 'L0_ffn_router_w': _L0_ffn_in['router_w'], 'L0_ffn_w_gate': _L0_ffn_in['w_gate'], 'L0_ffn_w_up': _L0_ffn_in['w_up'], 'L0_ffn_w_down': _L0_ffn_in['w_down'], 'L0_ffn_sw_gate': _L0_ffn_in['sw_gate'], 'L0_ffn_sw_up': _L0_ffn_in['sw_up'], 'L0_ffn_sw_down': _L0_ffn_in['sw_down'], 'L0_ffn_shared_gate_w': _L0_ffn_in['shared_gate_w']}
    _x0 = _d['L0_attn_x']
    _d['L0_attn_x'] = jax.random.normal(jax.random.fold_in(jax.random.key(seed), 1), (1, 2048, 256), dtype=_x0.dtype)
    del _x0
    return _d

def reference(L0_attn_x, L0_attn_Wq, L0_attn_Wk, L0_attn_Wv, L0_attn_Wo, L0_attn_conv_w, L0_attn_conv_b, L0_attn_Wig, L0_attn_big, L0_attn_Wog, L0_attn_bog, L0_attn_Wg, L0_attn_bg, L0_attn_vnw, L0_attn_vnb, L0_attn_mnw, L0_attn_mnb, L0_attn_gnw, L0_attn_gnb, L0_attn_ln1w, L0_attn_ln1b, L0_attn_ln2w, L0_attn_ln2b, L0_attn_Wgate, L0_attn_Wval, L0_attn_Wout, L0_ffn_router_w, L0_ffn_w_gate, L0_ffn_w_up, L0_ffn_w_down, L0_ffn_sw_gate, L0_ffn_sw_up, L0_ffn_sw_down, L0_ffn_shared_gate_w):

    def _L0_attn_ref(x, Wq, Wk, Wv, Wo, conv_w, conv_b, Wig, big, Wog, bog, Wg, bg, vnw, vnb, mnw, mnb, gnw, gnb, ln1w, ln1b, ln2w, ln2b, Wgate, Wval, Wout):
        import jax, jax.numpy as jnp
        import numpy as np
        D_MODEL = 256
        N_HEADS = 16
        HEAD_DIM = D_MODEL // N_HEADS
        FF = 1024
        KCONV = 4
        EPS = 1e-05

        def _layernorm(x, w, b, eps=EPS):
            m = jnp.mean(x, axis=-1, keepdims=True)
            v = jnp.mean(jnp.square(x - m), axis=-1, keepdims=True)
            return (x - m) * jax.lax.rsqrt(v + eps) * w + b

        def _long_block(x, Wq, Wk, Wv, Wo, conv_w, conv_b, Wig, big, Wog, bog, Wg, bg, vnw, vnb, mnw, mnb, gnw, gnb, ln1w, ln1b, ln2w, ln2b, Wgate, Wval, Wout):
            B, T, C = x.shape
            H, D = (N_HEADS, HEAD_DIM)
            h = _layernorm(x, ln1w, ln1b)
            ht = jnp.transpose(h, (0, 2, 1))
            xc = jax.lax.conv_general_dilated(ht, conv_w, window_strides=(1,), padding=[(KCONV - 1, 0)], dimension_numbers=('NCH', 'OIH', 'NCH'), feature_group_count=C) + conv_b[None, :, None]
            x_conv = jax.nn.silu(jnp.transpose(xc, (0, 2, 1)))

            def l2norm(t):
                return t * jax.lax.rsqrt(jnp.sum(t * t, axis=-1, keepdims=True) + 1e-12)
            q = l2norm((h @ Wq).reshape(B, T, H, D))
            k = l2norm((h @ Wk).reshape(B, T, H, D))
            v = _layernorm((h @ Wv).reshape(B, T, H, D), vnw, vnb)
            i_gate = jax.nn.sigmoid(x_conv @ Wig + big).reshape(B, T, H, D)
            gamma = jax.nn.sigmoid(x_conv @ Wg + bg).reshape(B, T, H, 1)
            u = i_gate * k * v
            g = jnp.broadcast_to(gamma, u.shape)

            def combine(c1, c2):
                a1, b1 = c1
                a2, b2 = c2
                return (a1 * a2, a2 * b1 + b2)
            _, mem = jax.lax.associative_scan(combine, (g, u), axis=1)
            out = (_layernorm(mem, mnw, mnb) * q).reshape(B, T, C)
            og = out.reshape(B, T, H, D)
            m = jnp.mean(og, axis=-1, keepdims=True)
            var = jnp.mean(jnp.square(og - m), axis=-1, keepdims=True)
            og = (og - m) * jax.lax.rsqrt(var + EPS)
            out = (og * gnw.reshape(H, D) + gnb.reshape(H, D)).reshape(B, T, C)
            out = out * jax.nn.sigmoid(x_conv @ Wog + bog)
            h = x + out @ Wo
            h2 = _layernorm(h, ln2w, ln2b)
            mlp = jax.nn.silu(h2 @ Wgate) * (h2 @ Wval) @ Wout
            return h + mlp
        return _long_block(x, Wq, Wk, Wv, Wo, conv_w, conv_b, Wig, big, Wog, bog, Wg, bg, vnw, vnb, mnw, mnb, gnw, gnb, ln1w, ln1b, ln2w, ln2b, Wgate, Wval, Wout)

    def _L0_ffn_ref(hidden_states, router_w, w_gate, w_up, w_down, sw_gate, sw_up, sw_down, shared_gate_w):
        import jax, jax.numpy as jnp
        import numpy as np
        E = 8
        TOP_K = 2
        H = 256
        I = 176
        SI = 704
        B, S, Hd = hidden_states.shape
        x = hidden_states.reshape(-1, Hd)
        shared = jnp.einsum('ts,sh->th', jax.nn.silu(x @ sw_gate) * (x @ sw_up), sw_down)
        logits = x @ router_w.T
        probs = jax.nn.softmax(logits.astype(jnp.float32), axis=-1)
        top_w, top_i = jax.lax.top_k(probs, TOP_K)
        top_w = top_w / jnp.sum(top_w, axis=-1, keepdims=True)
        combine = jnp.sum(jax.nn.one_hot(top_i, E, dtype=x.dtype) * top_w[..., None].astype(x.dtype), axis=1)
        h = jax.nn.silu(jnp.einsum('th,ehi->eti', x, w_gate)) * jnp.einsum('th,ehi->eti', x, w_up)
        expert_out = jnp.einsum('eti,eih->eth', h, w_down)
        routed = jnp.einsum('eth,te->th', expert_out, combine)
        shared_out = jax.nn.sigmoid(x @ shared_gate_w)[:, None] * shared
        return (routed + shared_out).reshape(B, S, Hd)
    x = L0_attn_x
    x = x + _layernorm(_L0_attn_ref(_layernorm(x, axis=-1), L0_attn_Wq, L0_attn_Wk, L0_attn_Wv, L0_attn_Wo, L0_attn_conv_w, L0_attn_conv_b, L0_attn_Wig, L0_attn_big, L0_attn_Wog, L0_attn_bog, L0_attn_Wg, L0_attn_bg, L0_attn_vnw, L0_attn_vnb, L0_attn_mnw, L0_attn_mnb, L0_attn_gnw, L0_attn_gnb, L0_attn_ln1w, L0_attn_ln1b, L0_attn_ln2w, L0_attn_ln2b, L0_attn_Wgate, L0_attn_Wval, L0_attn_Wout), axis=-1)
    x = x + _layernorm(_L0_ffn_ref(_layernorm(x, axis=-1), L0_ffn_router_w, L0_ffn_w_gate, L0_ffn_w_up, L0_ffn_w_down, L0_ffn_sw_gate, L0_ffn_sw_up, L0_ffn_sw_down, L0_ffn_shared_gate_w), axis=-1)
    return x

_drawn_inputs = setup_inputs


def setup_inputs(seed=0):
    import zlib

    import numpy as np

    out = dict(_drawn_inputs(seed))
    spreads = {'L0_attn_conv_b': (0.0, 0.1),
     'L0_attn_Wig': (0.0, 0.1),
     'L0_attn_big': (-3.0, 0.2),
     'L0_attn_bog': (0.0, 0.1),
     'L0_attn_Wg': (0.0, 0.1),
     'L0_attn_vnw': (1.0, 0.2),
     'L0_attn_vnb': (0.0, 0.1),
     'L0_attn_mnw': (1.0, 0.2),
     'L0_attn_mnb': (0.0, 0.1),
     'L0_attn_gnw': (1.0, 0.2),
     'L0_attn_gnb': (0.0, 0.1),
     'L0_attn_ln1w': (1.0, 0.2),
     'L0_attn_ln1b': (0.0, 0.1),
     'L0_attn_ln2w': (1.0, 0.2),
     'L0_attn_ln2b': (0.0, 0.1)}
    factors = {}
    for name, (base, spread) in spreads.items():
        noise = np.random.default_rng([zlib.crc32(name.encode()), seed]).standard_normal(out[name].shape)
        drawn = base * np.exp(spread * noise) if base else spread * noise
        out[name] = jnp.asarray(drawn.astype(out[name].dtype))
    for name, factor in factors.items():
        out[name] = (out[name] * factor).astype(out[name].dtype)
    return out
```

```python
from contextlib import ExitStack

import numpy as np

import concourse.bass as bass
from concourse import mybir

P = 128
T, D = 2048, 256
C = D // P
TB = 512
NB = T // TB
J = TB // P
NT = T // P
HEADS, HD = 16, 16
FF = 1024
FM = FF // P
KC = 4
E, EI, SI = 8, 176, 704
SL = SI // EI
NE = E + SL
PAIRS = NE // 2
PW = 2 * EI
PK = (PW + P - 1) // P
LASTK = PW - (PK - 1) * P
RW = 16
EPS = 1e-5

F32, F32R, I32 = mybir.dt.float32, mybir.dt.float32r, mybir.dt.int32
ALU = mybir.AluOpType
ACT = mybir.ActivationFunctionType
AX_X = mybir.AxisListType.X

LN1W, LN1B, CONVW, CONVB, BIG, BOG, BG, GNW, GNB, LN2W, LN2B = 0, 1, 2, 6, 7, 8, 9, 10, 11, 12, 13
NVEC = 14


def build(nc, x, wq, wk, wv, wig, wog, wo, wg, wgate, wval, wout, vecs, headvecs, router, up, down, out):
    ctx = ExitStack()
    phase_a = ExitStack()
    with ctx:
        def sem(name):
            return ctx.enter_context(nc.semaphore(name))

        def sb(name, shape, dt=F32):
            return ctx.enter_context(nc.sbuf_tensor(name, shape, dt))

        def sba(name, shape, dt=F32):
            return phase_a.enter_context(nc.sbuf_tensor(name, shape, dt))

        psum = ctx.enter_context(nc.psum_tensor("psum", [P, 8, 512], F32))
        p_main, p_side = psum[:, 0:2, :], psum[:, 2:4, :]
        p_gate, p_val, p_down = psum[:, 4, :], psum[:, 5, :], psum[:, 6:8, :]

        X = sb("X", [P, NT, D])
        XTH = sb("XTH", [P, C, T], F32R)
        XTL = sb("XTL", [P, C, T], F32R)
        LG = sb("LG", [P, NT, RW])
        ident = sb("ident", [P, P])
        vec = sb("vec", [P, C, NVEC])
        hvec = sb("hvec", [P, 4, HD])
        cw = sb("cw", [P, NT, NE])
        wrH, wrL = sb("wrH", [P, C, RW], F32R), sb("wrL", [P, C, RW], F32R)
        st = sb("st", [P, J, 6])
        mv = sb("mv", [P, J, 2])
        va = sb("va", [P, J * 3 * HEADS])
        rs = sb("rs", [P, J * 3 * HEADS])
        rt = sb("rt", [P, J * 3 * HEADS])
        r1 = sb("r1", [P, J])
        nm = sb("nm", [P, J])

        qkvH, qkvL = sba("qkvH", [P, C, 3 * D], F32R), sba("qkvL", [P, C, 3 * D], F32R)
        gwH, gwL = sba("gwH", [P, C, 2 * D], F32R), sba("gwL", [P, C, 2 * D], F32R)
        woH, woL = sba("woH", [P, C, D], F32R), sba("woL", [P, C, D], F32R)
        gmH, gmL = sba("gmH", [P, C, D], F32R), sba("gmL", [P, C, D], F32R)
        wgtH, wgtL = sba("wgtH", [P, C, FF], F32R), sba("wgtL", [P, C, FF], F32R)
        wvlH, wvlL = sba("wvlH", [P, C, FF], F32R), sba("wvlL", [P, C, FF], F32R)
        wouH, wouL = sba("wouH", [P, FM, D], F32R), sba("wouL", [P, FM, D], F32R)
        raw = sba("raw", [P, 2, 1024])
        smallraw = sba("smallraw", [P, 2, C, RW])
        wmean = sba("wmean", [P, C, HEADS])
        Y0 = sba("Y0", [P, J, D])
        HN = sba("HN", [P, J, D])
        HT = sba("HT", [P, C, KC - 1 + TB])
        AH, AL = sba("AH", [P, C, TB], F32R), sba("AL", [P, C, TB], F32R)
        QKV = sba("QKV", [P, J, 3 * D])
        XC = sba("XC", [P, C, TB])
        IG, OG, GA = sba("IG", [P, C, TB]), sba("OG", [P, C, TB]), sba("GA", [P, C, TB])
        HR = sba("HR", [P, J, D])
        SQ = [G[:, :, :].rearrange("p c t -> p (c t)")[:, 0:3 * D] for G in (IG, OG)]
        MSQ = IG[:, :, :].rearrange("p c t -> p (c t)")
        H2H, H2L = sba("H2H", [P, C, TB], F32R), sba("H2L", [P, C, TB], F32R)
        SM, HM = raw[:, :, 0:TB], raw[:, :, TB:2 * TB]
        HMH, HML = sba("HMH", [P, 2, TB], F32R), sba("HML", [P, 2, TB], F32R)
        rr = sba("rr", [P, J, 3 * HEADS])
        mu = sba("mu", [P, J * HEADS])
        carry = sba("carry", [P, C])
        phase_a.close()

        upH, upL = sb("upH", [P, 2, C, 2 * PW], F32R), sb("upL", [P, 2, C, 2 * PW], F32R)
        dnH, dnL = sb("dnH", [P, 2, PK, D], F32R), sb("dnL", [P, 2, PK, D], F32R)
        upR, dnR = sb("upR", [P, C, 2 * PW]), sb("dnR", [P, PK, D])
        sg = sb("sg", [P, 2, PW])
        hb = sb("hb", [P, 2, PK * P])
        htH, htL = sb("htH", [P, 2, PK * P], F32R), sb("htL", [P, 2, PK * P], F32R)
        acc = sb("acc", [P, NT, D])
        rank = sb("rank", [P, E])
        ex, key = sb("ex", [P, NT, E]), sb("key", [P, NT, E])
        pick = sb("pick", [P, 2, NT, E])
        top = sb("top", [P, 4, NT])

        x_in = [sem(f"x_in{b}") for b in range(NB)]
        const_in, stored = sem("const_in"), sem("stored")
        w_in = [sem(f"w_in{i}") for i in range(9)]
        pair_in = [sem(f"pair_in{i}") for i in range(2)]
        w_centred, w_hi, w_lo, small_ready = sem("w_centred"), sem("w_hi"), sem("w_lo"), sem("small_ready")
        ident_zero, ident_ready, halo_zero = sem("ident_zero"), sem("ident_ready"), sem("halo_zero")
        s_dve, s_act, s_pool = sem("s_dve"), sem("s_act"), sem("s_pool")
        y0_ready, hn_ready, ht_psum, ht_ready, ht_hi, ht_lo = map(
            sem, ("y0_ready", "hn_ready", "ht_psum", "ht_ready", "ht_hi", "ht_lo"))
        conv_done, conv_hi, conv_lo = map(sem, ("conv_done", "conv_hi", "conv_lo"))
        qkv_psum, qkv_copied, sq_ready, ss_done, v_scaled = map(
            sem, ("qkv_psum", "qkv_copied", "sq_ready", "ss_done", "v_scaled"))
        gate_psum, gate_ready = sem("gate_psum"), sem("gate_ready")
        rr_ready, u_ready, g_ready, ut_psum, mem_ready, mem_psum = map(
            sem, ("rr_ready", "u_ready", "g_ready", "ut_psum", "mem_ready", "mem_psum"))
        centred, msq_ready, og_ready, og_psum, og_affine, o_ready, o_hi, o_lo = map(
            sem, ("centred", "msq_ready", "og_ready", "og_psum", "og_affine", "o_ready", "o_hi", "o_lo"))
        wo_psum, hr_ready, ln2_stats, hn2_ready, h2_psum, h2_hi, h2_lo = map(
            sem, ("wo_psum", "hr_ready", "ln2_stats", "hn2_ready", "h2_psum", "h2_hi", "h2_lo"))
        up_psum, silu_ready, hid_ready, hid_hi, hid_lo, down_psum = map(
            sem, ("up_psum", "silu_ready", "hid_ready", "hid_hi", "hid_lo", "down_psum"))
        x2_stats, xn_ready, xt_psum, xt_hi, xt_lo, rt_psum, rt_copied = map(
            sem, ("x2_stats", "xn_ready", "xt_psum", "xt_hi", "xt_lo", "rt_psum", "rt_copied"))
        lmax_ready, exp_ready, cw_ready, pad_zero = map(sem, ("lmax_ready", "exp_ready", "cw_ready", "pad_zero"))
        pair_hi, pair_lo = sem("pair_hi"), sem("pair_lo")
        eup_psum, esilu_ready, ehid_ready, eht_psum, eht_hi, eht_lo, edown_psum, eacc_done = map(
            sem, ("eup_psum", "esilu_ready", "ehid_ready", "eht_psum", "eht_hi", "eht_lo", "edown_psum", "eacc_done"))
        out_ready = sem("out_ready")

        def f32(ap):
            return ap.bitcast(F32)

        def heads(ap, j=J):
            return ap.rearrange("p j (h d) -> p j h d", d=HD)

        def per_head(ap, j=J):
            return ap.unsqueeze(3).broadcast_to([P, j, HEADS, HD])

        def per_dim(i, j=J):
            return hvec[:, i, :].unsqueeze(1).unsqueeze(1).broadcast_to([P, j, HEADS, HD])

        def per_dim1(i):
            return hvec[:, i, :].unsqueeze(1).broadcast_to([P, HEADS, HD])

        v = lambda c, i: vec[:, c, i:i + 1]

        slot = [raw[:, i, :] for i in range(2)]

        def two(s, w):
            return s[:, 0:C * w].rearrange("p (c n) -> p c n", c=C)

        rows = lambda w: w.rearrange("(c p) n -> p c n", p=P)
        weights = []
        weights.append(([(two(slot[0], 2 * D)[:, :, 0:D], rows(wq)), (two(slot[0], 2 * D)[:, :, D:2 * D], rows(wk))],
                        two(slot[0], 2 * D), qkvH[:, :, 0:2 * D], qkvL[:, :, 0:2 * D]))
        weights.append(([(two(slot[1], D), rows(wv))], two(slot[1], D), qkvH[:, :, 2 * D:3 * D], qkvL[:, :, 2 * D:3 * D]))
        weights.append(([(two(slot[0], 2 * D)[:, :, 0:D], rows(wig)), (two(slot[0], 2 * D)[:, :, D:2 * D], rows(wog))],
                        two(slot[0], 2 * D), gwH[:, :, :], gwL[:, :, :]))
        weights.append(([(two(slot[1], D), rows(wo))], two(slot[1], D), woH[:, :, :], woL[:, :, :]))
        for dst_h, dst_l, w in ((wgtH, wgtL, wgate), (wvlH, wvlL, wval)):
            for c in range(C):
                s = slot[len(weights) % 2]
                weights.append(([(s, w[c * P:(c + 1) * P, :])], s, dst_h[:, c, :], dst_l[:, c, :]))
        for h in range(2):
            s = slot[len(weights) % 2].rearrange("p (m n) -> p m n", n=D)
            m0 = h * FM // 2
            weights.append(([(s, wout[m0 * P:(m0 + FM // 2) * P, :].rearrange("(m p) n -> p m n", p=P))], s,
                            wouH[:, m0:m0 + FM // 2, :], wouL[:, m0:m0 + FM // 2, :]))
        NW = len(weights)
        while len(w_in) < NW:
            w_in.append(sem(f"w_in{len(w_in)}"))
        W_QKV, W_GATES, W_O, W_UP, W_OUT = 2, 3, 4, 8, 10

        def schedule(b, at):
            between = {"a2": [0, 1], "a3": [2, 3], "a5": [4], "a6": [5], "a7": [6], "a8": [7]}
            for stage in ("a1", "a2", "a3", "a5", "a6", "a7", "a8", "a9", "a10", "a11"):
                if b < NB:
                    at(stage, b, None)
                if b > 0:
                    for m in between.get(stage, ()):
                        at("mlp", b - 1, m)
                    if stage == "a8":
                        at("end", b - 1, None)

        block = ctx.enter_context(nc.Block())

        @block.sync
        def _(sp):
            def load_x(b):
                sp.dma_start(X[:, b * J:(b + 1) * J, :],
                             x[b * TB:(b + 1) * TB, :].rearrange("(j p) d -> p j d", p=P)).then_inc(x_in[b], 16)

            def load_w(i):
                for dst, src in weights[i][0]:
                    sp.dma_start(dst, src).then_inc(w_in[i], 16)

            load_x(0)
            load_w(0)
            load_w(1)
            sp.dma_start(vec[:, :, :], vecs).then_inc(const_in, 16)
            sp.dma_start(hvec[:, :, :], headvecs).then_inc(const_in, 16)
            sp.dma_start(smallraw[:, 0, :, :], rows(wg)).then_inc(const_in, 16)
            sp.dma_start(smallraw[:, 1, :, :], router).then_inc(const_in, 16)
            for b in range(1, NB):
                load_x(b)
            for i in range(2, NW):
                sp.wait_ge(w_lo, i - 1)
                load_w(i)
            sp.wait_ge(xt_lo, C * NB)
            sp.wait_ge(rt_copied, NB)
            for p in range(PAIRS):
                if p > 0:
                    sp.wait_ge(pair_lo, 2 * p)
                sp.dma_start(upR[:, :, :], up[p]).then_inc(pair_in[p % 2], 16)
                sp.dma_start(dnR[:, 0:PK - 1, :],
                             down[p, 0:(PK - 1) * P, :].rearrange("(k p) n -> p k n", p=P)).then_inc(pair_in[p % 2], 16)
                sp.dma_start(dnR[0:LASTK, PK - 1, :], down[p, (PK - 1) * P:PW, :]).then_inc(pair_in[p % 2], 16)
            for g in range(NB):
                sp.wait_ge(out_ready, J * (g + 1))
                sp.dma_start(out[g * TB:(g + 1) * TB, :].rearrange("(j p) d -> p j d", p=P),
                             acc[:, g * J:(g + 1) * J, :]).then_inc(stored, 16)
            sp.wait_ge(stored, 16 * NB)

        @block.gpsimd
        def _(pool):
            n_pool = [0]

            def link(ins):
                n_pool[0] += 1
                ins.then_inc(s_pool, 1)
                pool.wait_ge(s_pool, n_pool[0])

            nc.gpsimd.memset(ident[:, :], 0.0).then_inc(ident_zero, 1)
            pool.wait_ge(ident_zero, 1)
            nc.gpsimd.affine_select(out=ident[:, :], in_=ident[:, :], compare_op=ALU.not_equal, fill=1.0, base=0,
                                    pattern=[[-1, P]], channel_multiplier=1).then_inc(ident_ready, 1)

            def split(i):
                pool.wait_ge(w_hi, i + 1)
                _, src, hi, lo = weights[i]
                nc.gpsimd.tensor_tensor(lo, src, f32(hi), ALU.subtract).then_inc(w_lo, 1)

            split(0)
            split(1)

            def at(stage, b, m):
                if stage == "a2":
                    for c in range(C):
                        pool.wait_ge(ht_hi, C * b + c + 1)
                        nc.gpsimd.tensor_tensor(AL[:, c, :], HT[:, c, KC - 1:], f32(AH[:, c, :]),
                                                ALU.subtract).then_inc(ht_lo, 1)
                    if b == 0:
                        split(2)
                        split(3)
                if stage == "a3":
                    for j in range(J):
                        pool.wait_ge(sq_ready, J * b + j + 1)
                        vj = QKV[:, j, 2 * D:3 * D].rearrange("p (h d) -> p h d", d=HD)
                        nc.gpsimd.tensor_tensor(vj, vj, per_dim1(0), ALU.mult).then_inc(v_scaled, 1)
                    for c in range(C):
                        pool.wait_ge(conv_hi, C * b + c + 1)
                        nc.gpsimd.tensor_tensor(AL[:, c, :], XC[:, c, :], f32(AH[:, c, :]),
                                                ALU.subtract).then_inc(conv_lo, 1)
                    if b == 0:
                        for i in range(4, NW):
                            split(i)
                if stage == "a6":
                    q, k, w = (heads(QKV[:, :, i * D:(i + 1) * D]) for i in range(3))
                    pool.wait_ge(rr_ready, b + 1)
                    link(nc.gpsimd.tensor_tensor(q, q, per_head(rr[:, :, 0:HEADS]), ALU.mult))
                    pool.wait_ge(u_ready, b + 1)
                    nc.gpsimd.tensor_tensor(k, q, per_dim(2), ALU.mult).then_inc(g_ready, 1)
                    pool.wait_ge(ut_psum, b + 1)
                    nc.gpsimd.tensor_tensor(w, q, per_dim(3), ALU.mult).then_inc(g_ready, 1)
                if stage == "mlp":
                    n = FM * b + m
                    pool.wait_ge(hid_hi, n + 1)
                    nc.gpsimd.tensor_tensor(HML[:, n % 2, :], HM[:, n % 2, :], f32(HMH[:, n % 2, :]),
                                            ALU.subtract).then_inc(hid_lo, 1)

            for b in range(NB + 1):
                schedule(b, at)

            for p in range(PAIRS):
                i = p % 2
                pool.wait_ge(pair_hi, 3 * (p + 1))
                nc.gpsimd.tensor_tensor(upL[:, i], upR[:, :, :], f32(upH[:, i]), ALU.subtract).then_inc(pair_lo, 1)
                link(nc.gpsimd.tensor_tensor(dnL[:, i, 0:PK - 1], dnR[:, 0:PK - 1, :], f32(dnH[:, i, 0:PK - 1]),
                                             ALU.subtract))
                nc.gpsimd.tensor_tensor(dnL[0:LASTK, i, PK - 1], dnR[0:LASTK, PK - 1, :],
                                        f32(dnH[0:LASTK, i, PK - 1]), ALU.subtract).then_inc(pair_lo, 1)

        @block.scalar
        def _(act):
            n_act = [0]

            def step(ins):
                n_act[0] += 1
                ins.then_inc(s_act, 1)

            def settle():
                act.wait_ge(s_act, n_act[0])

            def split(i):
                act.wait_ge(w_in[i], 16 * len(weights[i][0]))
                if i == 1:
                    act.wait_ge(w_centred, 1)
                nc.scalar.activation(weights[i][2], weights[i][1], ACT.Copy).then_inc(w_hi, 1)

            split(0)

            def at(stage, b, m):
                if stage == "a1":
                    for j in range(J):
                        act.wait_ge(y0_ready, J * b + j + 1)
                        if b > 0 and j == 0:
                            act.wait_ge(h2_psum, b)
                        nc.scalar.activation(HN[:, j, :], Y0[:, j, :], ACT.Copy,
                                             scale=r1[:, j:j + 1]).then_inc(hn_ready, 1)
                    if b == 0:
                        split(1)
                if stage == "a2":
                    if b == 0:
                        act.wait_ge(const_in, 64)
                        act.wait_ge(halo_zero, 1)
                    else:
                        act.wait_ge(conv_done, C * b)
                        act.wait_ge(ht_lo, C * b)
                        step(nc.scalar.activation(HT[:, :, 0:KC - 1], HT[:, :, TB:TB + KC - 1], ACT.Copy))
                        settle()
                    act.wait_ge(ht_psum, b + 1)
                    for c in range(C):
                        nc.scalar.activation(HT[:, c, KC - 1:], p_main[:, c, :], ACT.Identity, bias=v(c, LN1B),
                                             scale=v(c, LN1W)).then_inc(ht_ready, 1)
                    if b > 0:
                        act.wait_ge(wo_psum, b)
                    for c in range(C):
                        act.wait_ge(ht_ready, C * b + c + 1)
                        nc.scalar.activation(AH[:, c, :], HT[:, c, KC - 1:], ACT.Copy).then_inc(ht_hi, 1)
                    if b == 0:
                        split(2)
                        split(3)
                if stage == "a3":
                    for j in range(J):
                        n = J * b + j
                        act.wait_ge(qkv_psum, n + 1)
                        src = (p_side if j % 2 == 0 else p_main).rearrange("p a n -> p (a n)")[:, 0:3 * D]
                        nc.scalar.activation(QKV[:, j, :], src, ACT.Copy).then_inc(qkv_copied, 1)
                        act.wait_ge(qkv_copied, n + 1)
                        if n >= 2:
                            act.wait_ge(ss_done, n - 1)
                        nc.scalar.activation(SQ[n % 2], QKV[:, j, :], ACT.Square).then_inc(sq_ready, 1)
                    for c in range(C):
                        act.wait_ge(conv_done, C * b + c + 1)
                        step(nc.scalar.activation(XC[:, c, :], XC[:, c, :], ACT.Silu))
                    settle()
                    for c in range(C):
                        nc.scalar.activation(AH[:, c, :], XC[:, c, :], ACT.Copy).then_inc(conv_hi, 1)
                    if b == 0:
                        for i in range(4, NW):
                            split(i)
                if stage == "a5":
                    for g, (dst, bias) in enumerate(((IG, BIG), (OG, BOG), (GA, BG))):
                        src = p_side if g == 1 else p_main
                        act.wait_ge(gate_psum, 3 * b + g + 1)
                        if g == 0:
                            act.wait_ge(ss_done, J * (b + 1))
                        if g == 0 and b > 0:
                            act.wait_ge(h2_lo, C * b)
                        for c in range(C):
                            nc.scalar.activation(dst[:, c, :], src[:, c, :], ACT.Sigmoid,
                                                 bias=v(c, bias)).then_inc(gate_ready, 1)
                if stage == "a8":
                    for k in range(2):
                        act.wait_ge(centred, 2 * b + k + 1)
                        nc.scalar.activation(MSQ,
                                             HN[:, :, :].rearrange("p j d -> p (j d)"), ACT.Square).then_inc(msq_ready, 1)
                if stage == "a9":
                    act.wait_ge(og_psum, b + 1)
                    for c in range(C):
                        nc.scalar.activation(GA[:, c, :], p_main[:, c, :], ACT.Identity, bias=v(c, GNB),
                                             scale=v(c, GNW)).then_inc(og_affine, 1)
                    for c in range(C):
                        act.wait_ge(o_ready, C * b + c + 1)
                        nc.scalar.activation(AH[:, c, :], OG[:, c, :], ACT.Copy).then_inc(o_hi, 1)
                if stage == "a11":
                    act.wait_ge(ln2_stats, b + 1)
                    for j in range(J):
                        nc.scalar.activation(HN[:, j, :], HR[:, j, :], ACT.Identity, bias=nm[:, j:j + 1],
                                             scale=rs[:, j:j + 1]).then_inc(hn2_ready, 1)
                    act.wait_ge(h2_psum, b + 1)
                    for c in range(C):
                        step(nc.scalar.activation(GA[:, c, :], p_main[:, c, :], ACT.Identity, bias=v(c, LN2B),
                                                  scale=v(c, LN2W)))
                    settle()
                    if b > 0:
                        act.wait_ge(up_psum, FM * b)
                    for c in range(C):
                        nc.scalar.activation(H2H[:, c, :], GA[:, c, :], ACT.Copy).then_inc(h2_hi, 1)
                if stage == "mlp":
                    n = FM * b + m
                    act.wait_ge(up_psum, n + 1)
                    if n == 0:
                        act.wait_ge(w_lo, NW)
                    if n >= 2:
                        act.wait_ge(hid_ready, n - 1)
                    nc.scalar.activation(SM[:, n % 2, :], p_gate, ACT.Silu).then_inc(silu_ready, 1)
                    act.wait_ge(hid_ready, n + 1)
                    if n >= 2:
                        act.wait_ge(down_psum, n - 1)
                    nc.scalar.activation(HMH[:, n % 2, :], HM[:, n % 2, :], ACT.Copy).then_inc(hid_hi, 1)
                if stage == "end":
                    act.wait_ge(x2_stats, b + 1)
                    for j in range(J):
                        nc.scalar.activation(HR[:, j, :], X[:, b * J + j, :], ACT.Identity, bias=nm[:, j:j + 1],
                                             scale=rs[:, j:j + 1]).then_inc(xn_ready, 1)
                    act.wait_ge(xt_psum, b + 1)
                    for c in range(C):
                        nc.scalar.activation(XTH[:, c, b * TB:(b + 1) * TB], p_down[:, c, :],
                                             ACT.Copy).then_inc(xt_hi, 1)

            for b in range(NB + 1):
                schedule(b, at)

            def split_pair(p):
                i = p % 2
                act.wait_ge(pair_in[p % 2], 48 * (p // 2 + 1))
                if p >= 2:
                    act.wait_ge(edown_psum, NT * (p - 1))
                nc.scalar.activation(upH[:, i], upR[:, :, :], ACT.Copy).then_inc(pair_hi, 1)
                nc.scalar.activation(dnH[:, i, 0:PK - 1], dnR[:, 0:PK - 1, :], ACT.Copy).then_inc(pair_hi, 1)
                nc.scalar.activation(dnH[0:LASTK, i, PK - 1], dnR[0:LASTK, PK - 1, :], ACT.Copy).then_inc(pair_hi, 1)

            split_pair(0)
            act.wait_ge(lmax_ready, 1)
            nc.scalar.activation(ex[:, :, :], ex[:, :, :], ACT.Exp).then_inc(exp_ready, 1)
            for s in range(SL):
                nc.scalar.activation(cw[:, :, E + s], LG[:, :, E], ACT.Sigmoid).then_inc(exp_ready, 1)

            def turn(n):
                act.wait_ge(eht_psum, n + 1)
                if n >= 2:
                    act.wait_ge(edown_psum, n - 1)
                nc.scalar.activation(htH[:, n % 2, :], psum[:, 4 + n % 2, 0:PK * P], ACT.Copy).then_inc(eht_hi, 1)

            N = PAIRS * NT
            for n in range(N + 1):
                if n < N:
                    act.wait_ge(eup_psum, n + 1)
                    if n >= 2:
                        act.wait_ge(ehid_ready, 2 * (n - 1))
                    nc.scalar.activation(sg[:, n % 2, :], psum[:, 2 * (n % 2), 0:PW], ACT.Silu).then_inc(esilu_ready, 1)
                if n >= 1:
                    turn(n - 1)
                if n % NT == 2 and n // NT + 1 < PAIRS:
                    split_pair(n // NT + 1)

        @block.tensor
        def _(pe):
            def mm3(dst, aH, aL, bH, bL, start, stop, shared=False):
                nc.tensor.matmul(dst, aH, bH, start=start, stop=False, skip_group_check=shared)
                nc.tensor.matmul(dst, aH, bL, start=False, stop=False, skip_group_check=shared)
                return nc.tensor.matmul(dst, aL, bH, start=False, stop=stop, skip_group_check=shared)

            def to_features(dst, src):
                for c in range(C):
                    for j in range(J):
                        last = nc.tensor.transpose(dst[:, c, j * P:(j + 1) * P], src(j)[:, c * P:(c + 1) * P], ident[:, :])
                return last

            pe.wait_ge(ident_ready, 1)

            def mlp_up(n):
                m = n % FM
                if n >= 1:
                    pe.wait_ge(hid_ready, n)
                for dst, wH, wL in ((p_gate, wgtH, wgtL), (p_val, wvlH, wvlL)):
                    for c in range(C):
                        last = mm3(dst, wH[:, c, m * P:(m + 1) * P], wL[:, c, m * P:(m + 1) * P], H2H[:, c, :],
                                   H2L[:, c, :], c == 0, c == C - 1)
                last.then_inc(up_psum, 1)

            def mlp_down(n):
                m = n % FM
                pe.wait_ge(hid_lo, n + 1)
                for j in range(J):
                    cols = slice(j * P, (j + 1) * P)
                    last = mm3(p_down[:, j // 2, (j % 2) * D:(j % 2 + 1) * D], HMH[:, n % 2, cols], HML[:, n % 2, cols],
                               wouH[:, m, :], wouL[:, m, :], m == 0 and j % 2 == 0, m == FM - 1, shared=True)
                last.then_inc(down_psum, 1)

            def at(stage, b, m):
                if stage == "a2":
                    pe.wait_ge(hn_ready, J * (b + 1))
                    to_features(p_main, lambda j: HN[:, j, :]).then_inc(ht_psum, 1)
                if stage == "a3":
                    if b == 0:
                        pe.wait_ge(w_lo, W_QKV)
                    pe.wait_ge(ht_lo, C * (b + 1))
                    for j in range(J):
                        n = J * b + j
                        if j >= 2:
                            pe.wait_ge(qkv_copied, n - 1)
                        dst = p_side if j % 2 == 0 else p_main
                        cols = slice(j * P, (j + 1) * P)
                        for part, wcols in ((0, slice(0, 2 * D)), (1, slice(2 * D, 3 * D))):
                            width = wcols.stop - wcols.start
                            for c in range(C):
                                last = mm3(dst[:, part, 0:width], AH[:, c, cols], AL[:, c, cols], qkvH[:, c, wcols],
                                           qkvL[:, c, wcols], c == 0, c == C - 1)
                        last.then_inc(qkv_psum, 1)
                if stage == "a5":
                    pe.wait_ge(qkv_copied, J * (b + 1))
                    if b == 0:
                        pe.wait_ge(w_lo, W_GATES)
                        pe.wait_ge(small_ready, 4)
                    pe.wait_ge(conv_lo, C * (b + 1))
                    for g, (wH, wL, w0) in enumerate(((gwH, gwL, 0), (gwH, gwL, D), (gmH, gmL, 0))):
                        dst = p_side if g == 1 else p_main
                        if g == 2:
                            pe.wait_ge(gate_ready, 3 * C * b + C)
                        for o in range(C):
                            cols = slice(w0 + o * P, w0 + (o + 1) * P)
                            for c in range(C):
                                last = mm3(dst[:, o, :], wH[:, c, cols], wL[:, c, cols], AH[:, c, :], AL[:, c, :],
                                           c == 0, c == C - 1)
                        last.then_inc(gate_psum, 1)
                if stage == "a6":
                    pe.wait_ge(u_ready, b + 1)
                    pe.wait_ge(gate_ready, 3 * C * (b + 1))
                    to_features(p_main, lambda j: QKV[:, j, 2 * D:3 * D]).then_inc(ut_psum, 1)
                if stage == "a7":
                    pe.wait_ge(mem_ready, C * (b + 1))
                    for j in range(J):
                        for c in range(C):
                            last = nc.tensor.transpose(p_main[:, j // 2, (j % 2) * D + c * P:(j % 2) * D + (c + 1) * P],
                                                       IG[:, c, j * P:(j + 1) * P], ident[:, :])
                    last.then_inc(mem_psum, 1)
                if stage == "a9":
                    pe.wait_ge(og_ready, b + 1)
                    to_features(p_main, lambda j: HN[:, j, :]).then_inc(og_psum, 1)
                if stage == "a10":
                    if b == 0:
                        pe.wait_ge(w_lo, W_O)
                    pe.wait_ge(o_lo, C * (b + 1))
                    for j in range(J):
                        cols = slice(j * P, (j + 1) * P)
                        for c in range(C):
                            last = mm3(p_side[:, j // 2, (j % 2) * D:(j % 2 + 1) * D], AH[:, c, cols], AL[:, c, cols],
                                       woH[:, c, :], woL[:, c, :], c == 0, c == C - 1)
                    last.then_inc(wo_psum, 1)
                if stage == "a11":
                    pe.wait_ge(hn2_ready, J * (b + 1))
                    to_features(p_main, lambda j: HN[:, j, :]).then_inc(h2_psum, 1)
                if stage == "mlp":
                    n = FM * b + m
                    if m == 0:
                        pe.wait_ge(h2_lo, C * (b + 1))
                        if b == 0:
                            pe.wait_ge(w_lo, W_UP)
                        else:
                            pe.wait_ge(rt_copied, b)
                    mlp_up(n)
                    if m == 1:
                        if b == 0:
                            pe.wait_ge(w_lo, W_OUT)
                        else:
                            pe.wait_ge(xt_lo, C * b)
                    if m >= 1:
                        mlp_down(n - 1)
                    if m == FM - 1:
                        mlp_down(n)
                if stage == "end":
                    pe.wait_ge(xn_ready, J * (b + 1))
                    to_features(p_down, lambda j: HR[:, j, :]).then_inc(xt_psum, 1)
                    pe.wait_ge(xt_lo, C * (b + 1))
                    for j in range(J):
                        t = slice(b * TB + j * P, b * TB + (j + 1) * P)
                        for c in range(C):
                            last = mm3(p_gate[:, j * RW:(j + 1) * RW], XTH[:, c, t], XTL[:, c, t], wrH[:, c, :],
                                       wrL[:, c, :], c == 0, c == C - 1)
                    last.then_inc(rt_psum, 1)

            for b in range(NB + 1):
                schedule(b, at)

            def up_product(n):
                p, t = divmod(n, NT)
                if t == 0:
                    pe.wait_ge(pair_lo, 2 * (p + 1))
                if n >= 2:
                    pe.wait_ge(ehid_ready, 2 * (n - 1))
                elif n == 0:
                    pe.wait_ge(rt_copied, NB)
                cols = slice(t * P, (t + 1) * P)
                for half in range(2):
                    for c in range(C):
                        w = slice(half * PW, (half + 1) * PW)
                        last = mm3(psum[:, 2 * (n % 2) + half, 0:PW], XTH[:, c, cols], XTL[:, c, cols],
                                   upH[:, p % 2, c, w], upL[:, p % 2, c, w], c == 0, c == C - 1)
                last.then_inc(eup_psum, 1)

            def turn(n):
                pe.wait_ge(ehid_ready, 2 * (n + 1))
                if n >= 2:
                    pe.wait_ge(eht_lo, n - 1)
                elif n == 0:
                    pe.wait_ge(pad_zero, 1)
                for k in range(PK):
                    last = nc.tensor.transpose(psum[:, 4 + n % 2, k * P:(k + 1) * P], hb[:, n % 2, k * P:(k + 1) * P],
                                               ident[:, :])
                last.then_inc(eht_psum, 1)

            def down_product(n):
                p = n // NT
                pe.wait_ge(eht_lo, n + 1)
                if n >= 2:
                    pe.wait_ge(eacc_done, n - 1)
                for k in range(PK):
                    rws = P if k < PK - 1 else LASTK
                    hid = slice(k * P, (k + 1) * P)
                    last = mm3(psum[:, 6 + n % 2, 0:D], htH[0:rws, n % 2, hid], htL[0:rws, n % 2, hid],
                               dnH[0:rws, p % 2, k, :], dnL[0:rws, p % 2, k, :], k == 0, k == PK - 1)
                last.then_inc(edown_psum, 1)

            N = PAIRS * NT
            for n in range(N + 2):
                if n < N:
                    up_product(n)
                if 1 <= n <= N:
                    turn(n - 1)
                if n >= 2:
                    down_product(n - 2)

        @block.vector
        def _(dve):
            n_dve = [0]

            def step(ins):
                n_dve[0] += 1
                ins.then_inc(s_dve, 1)

            def settle():
                dve.wait_ge(s_dve, n_dve[0])

            def link(ins):
                step(ins)
                settle()

            def rsqrt(n):
                a, y, t = va[:, 0:n], rs[:, 0:n], rt[:, 0:n]
                link(nc.vector.tensor_scalar(y.bitcast(I32), a.bitcast(I32), 1, None, ALU.logical_shift_right))
                link(nc.vector.tensor_scalar(y.bitcast(I32), y.bitcast(I32), -1.0, float(0x5F3759DF), ALU.mult, ALU.add))
                for _ in range(3):
                    link(nc.vector.tensor_tensor(t, y, y, ALU.mult))
                    link(nc.vector.scalar_tensor_tensor(t, t, -0.5, a, ALU.mult, ALU.mult))
                    link(nc.vector.scalar_tensor_tensor(y, t, 1.5, y, ALU.add, ALU.mult))

            def stats(tile):
                for j in range(J):
                    step(nc.vector.bn_stats(st[:, j, :], tile(j)))
                settle()
                for j in range(J):
                    step(nc.vector.bn_aggr(mv[:, j, :], st[:, j, :]))
                settle()

            def rstd():
                link(nc.vector.tensor_scalar(va[:, 0:J], mv[:, :, 1], EPS, None, ALU.add))
                rsqrt(J)

            def minus_mean(done):
                nc.vector.scalar_tensor_tensor(nm[:, :], mv[:, :, 0], -1.0, rs[:, 0:J], ALU.mult,
                                               ALU.mult).then_inc(done, 1)

            step(nc.vector.memset(carry[:, :], 0.0))
            nc.vector.memset(HT[:, :, 0:KC - 1], 0.0).then_inc(halo_zero, 1)

            def prepare_weights():
                dve.wait_ge(w_in[1], 16)
                wv_raw = weights[1][1].rearrange("p c (h d) -> p c h d", d=HD)
                link(nc.vector.tensor_reduce(wmean[:, :, :], wv_raw, AX_X, ALU.add))
                link(nc.vector.tensor_scalar(wmean[:, :, :], wmean[:, :, :], -1.0 / HD, None, ALU.mult))
                nc.vector.tensor_tensor(wv_raw, wv_raw, wmean[:, :, :].unsqueeze(3).broadcast_to([P, C, HEADS, HD]),
                                        ALU.add).then_inc(w_centred, 1)
                dve.wait_ge(const_in, 64)
                wide = smallraw[:, 0, :, :].unsqueeze(3).broadcast_to([P, C, HEADS, HD])
                gm = lambda w: w[:, :, :].rearrange("p c (h d) -> p c h d", d=HD)
                nc.vector.tensor_copy(gm(gmH), wide).then_inc(small_ready, 1)
                nc.vector.tensor_copy(wrH[:, :, :], smallraw[:, 1, :, :]).then_inc(small_ready, 1)
                dve.wait_ge(small_ready, 2)
                nc.vector.tensor_tensor(gm(gmL), wide, f32(gm(gmH)), ALU.subtract).then_inc(small_ready, 1)
                nc.vector.tensor_tensor(wrL[:, :, :], smallraw[:, 1, :, :], f32(wrH[:, :, :]),
                                        ALU.subtract).then_inc(small_ready, 1)

            flat = lambda ap: ap.rearrange("p j d -> p (j d)")
            by_head = lambda ap: ap.rearrange("p (h d) -> p h d", d=HD)
            G = J * HEADS

            def spread(ap):
                return ap.unsqueeze(2).broadcast_to([P, G, HD])

            def centre(src):
                link(nc.vector.tensor_reduce(mu[:, :], by_head(src), AX_X, ALU.add))
                link(nc.vector.tensor_scalar(mu[:, :], mu[:, :], -1.0 / HD, None, ALU.mult))
                nc.vector.tensor_tensor(by_head(flat(HN[:, :, :])), by_head(src), spread(mu[:, :]),
                                        ALU.add).then_inc(centred, 1)

            def head_rstd(n):
                dve.wait_ge(msq_ready, n)
                link(nc.vector.tensor_reduce(va[:, 0:G], by_head(MSQ), AX_X, ALU.add))
                link(nc.vector.tensor_scalar(va[:, 0:G], va[:, 0:G], 1.0 / HD, EPS, ALU.mult, ALU.add))
                rsqrt(G)

            def at(stage, b, m):
                if stage == "a1":
                    dve.wait_ge(x_in[b], 16)
                    stats(lambda j: X[:, b * J + j, :])
                    rstd()
                    link(nc.vector.tensor_tensor(va[:, 0:J], mv[:, :, 1], rs[:, 0:J], ALU.mult))
                    link(nc.vector.tensor_tensor(va[:, 0:J], va[:, 0:J], rs[:, 0:J], ALU.mult))
                    link(nc.vector.tensor_scalar(va[:, 0:J], va[:, 0:J], EPS, None, ALU.add))
                    link(nc.vector.tensor_copy(r1[:, :], rs[:, 0:J]))
                    rsqrt(J)
                    link(nc.vector.tensor_copy(nm[:, :], r1[:, :]))
                    link(nc.vector.tensor_copy(r1[:, :], rs[:, 0:J]))
                    for j in range(J):
                        nc.vector.tensor_scalar(Y0[:, j, :], X[:, b * J + j, :], mv[:, j, 0:1], nm[:, j:j + 1],
                                                ALU.subtract, ALU.mult).then_inc(y0_ready, 1)
                    if b == 0:
                        prepare_weights()
                if stage == "a2":
                    if b > 0:
                        dve.wait_ge(conv_lo, C * b)
                    for c in range(C):
                        dve.wait_ge(ht_ready, C * b + c + 1)
                        step(nc.vector.tensor_scalar(XC[:, c, :], HT[:, c, 0:TB], v(c, CONVW), v(c, CONVB), ALU.mult,
                                                     ALU.add))
                    for k in range(1, KC):
                        settle()
                        for c in range(C):
                            ins = nc.vector.scalar_tensor_tensor(XC[:, c, :], HT[:, c, k:k + TB], v(c, CONVW + k),
                                                                 XC[:, c, :], ALU.mult, ALU.add)
                            if k < KC - 1:
                                step(ins)
                            else:
                                ins.then_inc(conv_done, 1)
                if stage == "a3":
                    for j in range(J):
                        n = J * b + j
                        dve.wait_ge(sq_ready, n + 1)
                        nc.vector.tensor_reduce(va[:, j * 3 * HEADS:(j + 1) * 3 * HEADS], by_head(SQ[n % 2]), AX_X,
                                                ALU.add).then_inc(ss_done, 1)
                    dve.wait_ge(ss_done, J * (b + 1))
                    sums = va[:, :].rearrange("p (j h) -> p j h", j=J)
                    step(nc.vector.tensor_scalar(sums[:, :, 0:2 * HEADS], sums[:, :, 0:2 * HEADS], 1e-12, None, ALU.add))
                    link(nc.vector.tensor_scalar(sums[:, :, 2 * HEADS:], sums[:, :, 2 * HEADS:], 1.0 / HD, EPS,
                                                 ALU.mult, ALU.add))
                    rsqrt(J * 3 * HEADS)
                    if b > 0:
                        dve.wait_ge(g_ready, 2 * b)
                    nc.vector.tensor_copy(rr[:, :, :], rs[:, :].rearrange("p (j h) -> p j h", j=J)).then_inc(rr_ready, 1)
                if stage == "a5":
                    k, w = heads(QKV[:, :, D:2 * D]), heads(QKV[:, :, 2 * D:3 * D])
                    dve.wait_ge(rr_ready, b + 1)
                    dve.wait_ge(v_scaled, J * (b + 1))
                    step(nc.vector.tensor_tensor(k, k, per_head(rr[:, :, HEADS:2 * HEADS]), ALU.mult))
                    link(nc.vector.tensor_tensor(w, w, per_head(rr[:, :, 2 * HEADS:]), ALU.mult))
                    link(nc.vector.tensor_tensor(w, w, per_dim(1), ALU.add))
                    nc.vector.tensor_tensor(w, w, k, ALU.mult).then_inc(u_ready, 1)
                if stage == "a7":
                    dve.wait_ge(gate_ready, 3 * C * (b + 1))
                    dve.wait_ge(ut_psum, b + 1)
                    for c in range(C):
                        step(nc.vector.tensor_tensor(IG[:, c, :], IG[:, c, :], p_main[:, c, :], ALU.mult))
                    settle()
                    for c in range(C):
                        nc.vector.tensor_tensor_scan(IG[:, c, :], GA[:, c, :], IG[:, c, :], carry[:, c:c + 1], ALU.mult,
                                                     ALU.add).then_inc(mem_ready, 1)
                    dve.wait_ge(mem_ready, C * (b + 1))
                    link(nc.vector.tensor_copy(carry[:, :], IG[:, :, TB - 1]))
                if stage == "a8":
                    dve.wait_ge(mem_psum, b + 1)
                    centre(flat(p_main))
                    m_flat = by_head(flat(HN[:, :, :]))
                    head_rstd(2 * b + 1)
                    link(nc.vector.tensor_tensor(m_flat, m_flat, spread(rs[:, 0:G]), ALU.mult))
                    dve.wait_ge(g_ready, 2 * (b + 1))
                    link(nc.vector.tensor_tensor(HN[:, :, :], HN[:, :, :], QKV[:, :, D:2 * D], ALU.mult))
                    link(nc.vector.tensor_tensor(HN[:, :, :], HN[:, :, :], QKV[:, :, 2 * D:], ALU.add))
                    centre(flat(HN[:, :, :]))
                    head_rstd(2 * b + 2)
                    nc.vector.tensor_tensor(m_flat, m_flat, spread(rs[:, 0:G]), ALU.mult).then_inc(og_ready, 1)
                if stage == "a9":
                    for c in range(C):
                        dve.wait_ge(og_affine, C * b + c + 1)
                        nc.vector.tensor_tensor(OG[:, c, :], OG[:, c, :], GA[:, c, :], ALU.mult).then_inc(o_ready, 1)
                    for c in range(C):
                        dve.wait_ge(o_hi, C * b + c + 1)
                        nc.vector.tensor_tensor(AL[:, c, :], OG[:, c, :], f32(AH[:, c, :]), ALU.subtract).then_inc(o_lo, 1)
                if stage == "a10":
                    dve.wait_ge(wo_psum, b + 1)
                    if b > 0:
                        dve.wait_ge(xt_psum, b)
                    nc.vector.tensor_tensor(flat(HR[:, :, :]), flat(p_side), flat(Y0[:, :, :]), ALU.add).then_inc(hr_ready, 1)
                if stage == "a11":
                    dve.wait_ge(hr_ready, b + 1)
                    stats(lambda j: HR[:, j, :])
                    rstd()
                    minus_mean(ln2_stats)
                    for c in range(C):
                        dve.wait_ge(h2_hi, C * b + c + 1)
                        nc.vector.tensor_tensor(H2L[:, c, :], GA[:, c, :], f32(H2H[:, c, :]), ALU.subtract).then_inc(h2_lo, 1)
                if stage == "mlp":
                    n = FM * b + m
                    dve.wait_ge(silu_ready, n + 1)
                    if n >= 2:
                        dve.wait_ge(hid_lo, n - 1)
                    nc.vector.tensor_tensor(HM[:, n % 2, :], SM[:, n % 2, :], p_val, ALU.mult).then_inc(hid_ready, 1)
                if stage == "end":
                    dve.wait_ge(down_psum, FM * (b + 1))
                    link(nc.vector.tensor_tensor(flat(HR[:, :, :]), flat(HR[:, :, :]), flat(p_down), ALU.add))
                    stats(lambda j: HR[:, j, :])
                    rstd()
                    for j in range(J):
                        step(nc.vector.tensor_scalar(HR[:, j, :], HR[:, j, :], mv[:, j, 0:1], rs[:, j:j + 1],
                                                     ALU.subtract, ALU.mult))
                    settle()
                    xb = X[:, b * J:(b + 1) * J, :]
                    link(nc.vector.tensor_tensor(xb, xb, HR[:, :, :], ALU.add))
                    stats(lambda j: X[:, b * J + j, :])
                    rstd()
                    minus_mean(x2_stats)
                    for c in range(C):
                        dve.wait_ge(xt_hi, C * b + c + 1)
                        t = slice(b * TB, (b + 1) * TB)
                        nc.vector.tensor_tensor(XTL[:, c, t], p_down[:, c, :], f32(XTH[:, c, t]),
                                                ALU.subtract).then_inc(xt_lo, 1)
                    dve.wait_ge(rt_psum, b + 1)
                    nc.vector.tensor_copy(LG[:, b * J:(b + 1) * J, :],
                                          p_gate[:, 0:J * RW].rearrange("p (j r) -> p j r", r=RW)).then_inc(rt_copied, 1)

            for b in range(NB + 1):
                schedule(b, at)

            def wide(ap):
                return ap.unsqueeze(2).broadcast_to([P, NT, E])

            nc.vector.memset(hb[:, :, PW:PK * P], 0.0).then_inc(pad_zero, 1)
            for e in range(E):
                step(nc.vector.memset(rank[:, e:e + 1], float(E - e)))
            dve.wait_ge(rt_copied, NB)
            link(nc.vector.tensor_reduce(top[:, 0, :], LG[:, :, 0:E], AX_X, ALU.max))
            nc.vector.tensor_tensor(ex[:, :, :], LG[:, :, 0:E], wide(top[:, 0, :]), ALU.subtract).then_inc(lmax_ready, 1)
            dve.wait_ge(exp_ready, 1 + SL)
            ranks = rank[:, :].unsqueeze(1).broadcast_to([P, NT, E])
            for i in range(2):
                src = ex if i == 0 else key
                link(nc.vector.tensor_reduce(top[:, 1, :], src[:, :, :], AX_X, ALU.max))
                link(nc.vector.tensor_tensor(pick[:, i], src[:, :, :], wide(top[:, 1, :]), ALU.is_equal))
                link(nc.vector.tensor_tensor(pick[:, i], pick[:, i], ranks, ALU.mult))
                link(nc.vector.tensor_reduce(top[:, 2, :], pick[:, i], AX_X, ALU.max))
                link(nc.vector.tensor_tensor(pick[:, i], pick[:, i], wide(top[:, 2, :]), ALU.is_equal))
                if i == 0:
                    link(nc.vector.scalar_tensor_tensor(key[:, :, :], pick[:, 0], -2.0, ex[:, :, :], ALU.mult, ALU.add))
            link(nc.vector.tensor_tensor(pick[:, 0], pick[:, 0], pick[:, 1], ALU.add))
            link(nc.vector.tensor_tensor(ex[:, :, :], ex[:, :, :], pick[:, 0], ALU.mult))
            link(nc.vector.tensor_reduce(top[:, 3, :], ex[:, :, :], AX_X, ALU.add))
            link(nc.vector.reciprocal(top[:, 3, :], top[:, 3, :]))
            nc.vector.tensor_tensor(cw[:, :, 0:E], ex[:, :, :], wide(top[:, 3, :]), ALU.mult).then_inc(cw_ready, 1)
            dve.wait_ge(cw_ready, 1)

            def hidden(n):
                p, t = divmod(n, NT)
                dve.wait_ge(esilu_ready, n + 1)
                if n >= 2:
                    dve.wait_ge(eht_psum, n - 1)
                for e in range(2):
                    cols = slice(e * EI, (e + 1) * EI)
                    nc.vector.scalar_tensor_tensor(hb[:, n % 2, cols], sg[:, n % 2, cols],
                                                   cw[:, t, 2 * p + e:2 * p + e + 1], psum[:, 2 * (n % 2) + 1, cols],
                                                   ALU.mult, ALU.mult).then_inc(ehid_ready, 1)

            def lo_part(n):
                dve.wait_ge(eht_hi, n + 1)
                if n >= 2:
                    dve.wait_ge(edown_psum, n - 1)
                nc.vector.tensor_tensor(htL[:, n % 2, :], psum[:, 4 + n % 2, 0:PK * P], f32(htH[:, n % 2, :]),
                                        ALU.subtract).then_inc(eht_lo, 1)

            def add_up(n):
                p, t = divmod(n, NT)
                dve.wait_ge(edown_psum, n + 1)
                y = psum[:, 6 + n % 2, 0:D]
                if p == 0:
                    nc.vector.tensor_copy(acc[:, t, :], y).then_inc(eacc_done, 1)
                else:
                    nc.vector.tensor_tensor(acc[:, t, :], acc[:, t, :], y, ALU.add).then_inc(eacc_done, 1)
                if p == PAIRS - 1 and t % J == J - 1:
                    finish(t // J)

            def finish(g):
                dve.wait_ge(eacc_done, (PAIRS - 1) * NT + (g + 1) * J)
                stats(lambda j: acc[:, g * J + j, :])
                rstd()
                for j in range(J):
                    a = acc[:, g * J + j, :]
                    step(nc.vector.tensor_scalar(a, a, mv[:, j, 0:1], rs[:, j:j + 1], ALU.subtract, ALU.mult))
                settle()
                for j in range(J):
                    t = g * J + j
                    nc.vector.tensor_tensor(acc[:, t, :], acc[:, t, :], X[:, t, :], ALU.add).then_inc(out_ready, 1)

            N = PAIRS * NT
            for n in range(N + 2):
                if n < N:
                    hidden(n)
                if 1 <= n <= N:
                    lo_part(n - 1)
                if n >= 2:
                    add_up(n - 2)


def kernel(**inputs):
    import concourse.bacc as bacc
    from concourse.bass_utils import run_bass_kernel_spmd

    a = {k: np.ascontiguousarray(val) for k, val in inputs.items()}
    A, M = "L0_attn_", "L0_ffn_"

    def features(u):
        return np.reshape(u, (C, P, -1)).transpose(1, 0, 2)

    vecs = np.concatenate([features(a[A + n]) for n in ("ln1w", "ln1b")]
                          + [features(a[A + "conv_w"][:, 0, :])]
                          + [features(a[A + n]) for n in ("conv_b", "big", "bog")]
                          + [features(np.repeat(a[A + "bg"], HD))]
                          + [features(a[A + n]) for n in ("gnw", "gnb", "ln2w", "ln2b")], axis=2)
    headvecs = np.stack([a[A + n] for n in ("vnw", "vnb", "mnw", "mnb")])
    headvecs = np.broadcast_to(headvecs[None], (P, 4, HD))
    router = np.concatenate([a[M + "router_w"].T, a[M + "shared_gate_w"][:, None],
                             np.zeros((D, RW - E - 1), np.float32)], axis=1)
    def pairs(w, shared):
        slices = shared.reshape(D, SL, EI).transpose(1, 0, 2)
        both = np.concatenate([w, slices], axis=0)
        return both.reshape(PAIRS, 2, D, EI).transpose(0, 2, 1, 3).reshape(PAIRS, D, PW)

    up = np.concatenate([pairs(a[M + "w_gate"], a[M + "sw_gate"]), pairs(a[M + "w_up"], a[M + "sw_up"])], axis=2)
    up = up.reshape(PAIRS, C, P, 2 * PW).transpose(0, 2, 1, 3)
    down = np.concatenate([a[M + "w_down"].reshape(E * EI, D), a[M + "sw_down"]], axis=0).reshape(PAIRS, PW, D)

    arrays = {
        "x": a[A + "x"].reshape(T, D), "wq": a[A + "Wq"], "wk": a[A + "Wk"], "wv": a[A + "Wv"],
        "wig": a[A + "Wig"], "wog": a[A + "Wog"], "wo": a[A + "Wo"], "wg": a[A + "Wg"],
        "wgate": a[A + "Wgate"], "wval": a[A + "Wval"], "wout": a[A + "Wout"],
        "vecs": vecs, "headvecs": headvecs, "router": features(router), "up": up, "down": down,
    }
    arrays = {k: np.ascontiguousarray(val) for k, val in arrays.items()}
    nc = bacc.Bacc("TRN2", target_bir_lowering=False, num_devices=1)
    args = [nc.dram_tensor(k, val.shape, mybir.dt.from_np(val.dtype), kind="ExternalInput").ap()
            for k, val in arrays.items()]
    args.append(nc.dram_tensor("out", (T, D), F32, kind="ExternalOutput").ap())
    build(nc, *args)
    r = run_bass_kernel_spmd(nc, [arrays], core_ids=[0])
    return r.results[0]["out"].reshape(1, T, D)
```

```python
from contextlib import ExitStack

import numpy as np

import concourse.bass as bass
from concourse import mybir

P = 128
T, D = 2048, 256
C = D // P
TB = 512
NB = T // TB
J = TB // P
NT = T // P
HEADS, HD = 16, 16
FF = 1024
FM = FF // P
KC = 4
E, EI, SI = 8, 176, 704
SL = SI // EI
NE = E + SL
PAIRS = NE // 2
PW = 2 * EI
PK = (PW + P - 1) // P
LASTK = PW - (PK - 1) * P
RW = E + 1
UNITS = PAIRS * J
EPS = 1e-5

F32, F32R, I32 = mybir.dt.float32, mybir.dt.float32r, mybir.dt.int32
ALU = mybir.AluOpType
ACT = mybir.ActivationFunctionType
AX_X = mybir.AxisListType.X

LN1W, LN1B, CONVW, CONVB, BIG, BOG, BG, GNW, GNB, LN2W, LN2B = 0, 1, 2, 6, 7, 8, 9, 10, 11, 12, 13
NVEC = 14


ATTENTION = (
    [("ln0", 0), ("ln0", 1), ("ln0", 2), ("ht", 0), ("ht", 1)] + [("conv", k) for k in range(KC)] + [("q", j) for j in range(J)]
    + [("xs", 0), ("xs", 1), ("rs", 0), ("rs", 1), ("g", 0), ("g", 1), ("g", 2)] + [("u", i) for i in range(4)]
    + [("ut", 0), ("scan", 0), ("scan", 1), ("mt", 0)]
    + [(s, 0) for s in ("mean", "centre", "var", "rstd", "norm")] + [("affine", 0), ("affine", 1)]
    + [(s, 1) for s in ("mean", "centre", "var", "rstd", "norm")]
    + [("og", 0), ("o", 0), ("o", 1), ("y0", 0), ("wo", 0), ("ln2", 0), ("ln2", 1), ("h2", 0), ("h2", 1)])


def _slot(k):
    steps = [("up", k)] if k < UNITS else []
    steps += [("turn", k - 1)] if 1 <= k <= UNITS else []
    steps += [("down", k - 2)] if k >= 2 else []
    if k % J == 1 and k > J:
        steps.append(("refill_up", k // J + 1))
    if k % J == 3 and k > J:
        steps.append(("refill_dn", k // J + 1))
    return steps


EXPERTS = ([("mup", 0)] + [s for m in range(1, FM) for s in (("mup", m), ("mdn", m - 1))] + [("mdn", FM - 1)]
           + [("sum", 0), ("sum", 1), ("x2", 0), ("x2", 1), ("xt", 0), ("route", 0), ("choose", 0), ("choose", 1), ("choose", 2),
              ("choose", 3)]
           + [s for k in range(UNITS + 2) for s in _slot(k)] + [("refill_dn", PAIRS + 1), ("finish", 0), ("finish", 1)])

PLACE = {
    "pe": [2, 4, 7, 11, 12, 13, 13, 13, 13, 14, 15, 17, 19, 19, 19, 19,
            20, 20, 21, 22, 22, 22, 25, 26, 28, 29, 29, 33, 34, 37, 37, 39,
            39, 39, 42, 64, 65, 76, 77, 77, 77, 78, 78, 78, 81, 92, 92, 103,
            108],
    "act": [-5, -4, 9, 10, 10, 11, 13, 18, 18, 19, 19, 19, 19, 19, 19, 19,
            19, 20, 22, 25, 35, 35, 35, 35, 35, 35, 35, 35, 37, 38, 48, 58,
            59, 59, 60, 60, 62, 62, 74, 74, 75, 75, 78, 80, 88, 96, 101, 105,
            107],
    "dve": [3, 4, 7, 9, 11, 12, 13, 14, 14, 15, 16, 20, 20, 20, 20, 20,
            20, 21, 21, 21, 21, 21, 23, 25, 26, 29, 29, 33, 33, 35, 38, 42,
            45, 49, 52, 55, 56, 62, 66, 73, 76, 77, 77, 77, 82, 87, 94, 102,
            107],
    "pool": [-42, -42, -2, -2, 10, 14, 20, 20, 20, 20, 20, 31, 37, 38, 38, 38,
            38, 38, 38, 38, 38, 38, 38, 38, 38, 38, 38, 38, 38, 39, 39, 41,
            51, 51, 51, 51, 55, 55, 55, 55, 55, 55, 55, 55, 55, 56, 56, 57,
            61],
}


def steps(engine):
    place = PLACE[engine]
    todo = [((b - 1) * len(EXPERTS) + place[i], s[0], b, s[1]) for b in range(NB) for i, s in enumerate(ATTENTION)]
    for n in range(NB * len(EXPERTS)):
        while todo and todo[0][0] <= n:
            yield todo.pop(0)[1:]
        name, m = EXPERTS[n % len(EXPERTS)]
        yield name, n // len(EXPERTS), m


def build(nc, x, wq, wk, wv, wig, wog, wo, wg, wgate, wval, wout, vecs, headvecs, router, up, down, out):
    ctx = ExitStack()
    with ctx:
        def sem(name):
            return ctx.enter_context(nc.semaphore(name))

        def sb(name, shape, dt=F32):
            return ctx.enter_context(nc.sbuf_tensor(name, shape, dt))

        psum = ctx.enter_context(nc.psum_tensor("psum", [P, 8, 512], F32))
        p_main, p_down = psum[:, 0:2, :], psum[:, 6:8, :]
        p_turn, p_part = psum[:, 6, 0:PK * P], psum[:, 7, 0:D]

        def p_pair(n):
            return psum[:, 2 + 2 * (n % 2), :], psum[:, 3 + 2 * (n % 2), :]

        shapes = {"qkv": [P, C, 3 * D], "gw": [P, C, 2 * D], "wo": [P, C, D], "wgt": [P, C, FF],
                  "wvl": [P, C, FF], "wou": [P, FM, D], "up": [P, 2, C, 2 * PW], "dn": [P, 2, PK, D],
                  "hm": [P, 2, TB]}
        with ExitStack() as first_names:
            raw = {k: first_names.enter_context(nc.sbuf_tensor(k + "R", s, F32)) for k, s in shapes.items()}
        lo = {k: sb(k + "L", s, F32R) for k, s in shapes.items()}
        hi = {k: sb(k + "H", s, F32R) for k, s in shapes.items()}

        ident = sb("ident", [P, P])
        vec = sb("vec", [P, C, NVEC])
        hvec = sb("hvec", [P, 4, HD])
        wr = sb("wr", [P, C, RW])
        wg16, wgx = sb("wg16", [P, C, HEADS]), sb("wgx", [P, C, D])
        wmean = sb("wmean", [P, C, HEADS])
        st, mv = sb("st", [P, J, 6]), sb("mv", [P, J, 2])
        est, emv = sb("est", [P, J, 6]), sb("emv", [P, J, 2])
        eva, ers, ert = (sb(k, [P, J]) for k in ("eva", "ers", "ert"))
        va, rs, rt = (sb(k, [P, J * 3 * HEADS]) for k in ("va", "rs", "rt"))
        r0, n0, s1, n1 = (sb(k, [P, J]) for k in ("r0", "n0", "s1", "n1"))
        l2r, l2n, x2r, x2n = (sb(k, [P, J]) for k in ("l2r", "l2n", "x2r", "x2n"))
        rr, mu, carry = sb("rr", [P, J, 3 * HEADS]), sb("mu", [P, J * HEADS]), sb("carry", [P, C])
        LG, ex, key = sb("LG", [P, J, RW]), sb("ex", [P, J, RW]), sb("key", [P, J, E])
        pick, top, rank = sb("pick", [P, 2, J, E]), sb("top", [P, 4, J]), sb("rank", [P, E])
        cw = sb("cw", [P, J, NE])
        X = sb("X", [P, 2, J, D])
        HN = sb("HN", [P, J, D])
        HT = sb("HT", [P, C, KC - 1 + TB])
        AH, AL = sb("AH", [P, C, TB], F32R), sb("AL", [P, C, TB], F32R)
        QKV = sb("QKV", [P, J, 3 * D])
        XC = sb("XC", [P, C, TB])
        IG, OG, GA = sb("IG", [P, C, TB]), sb("OG", [P, C, TB]), sb("GA", [P, C, TB])
        HR = sb("HR", [P, J, D])
        H2H, H2L = sb("H2H", [P, C, TB], F32R), sb("H2L", [P, C, TB], F32R)
        SQ = [G[:, :, :].rearrange("p c t -> p (c t)")[:, 0:3 * D] for G in (IG, OG)]
        MSQ = IG[:, :, :].rearrange("p c t -> p (c t)")
        XTH, XTL = sb("XTH", [P, C, TB], F32R), sb("XTL", [P, C, TB], F32R)
        hb = sb("hb", [P, 2, PK * P])
        htH, htL = sb("htH", [P, 2, PK * P], F32R), sb("htL", [P, 2, PK * P], F32R)
        acc = sb("acc", [P, J, D])

        SM, HMH, HML = raw["hm"], hi["hm"], lo["hm"]

        x_in = [sem(f"x_in{i}") for i in range(2)]
        const_in, stored = sem("const_in"), sem("stored")
        w_in = {k: sem(k + "_in") for k in ("qkv", "v", "gw", "wo", "wgt", "wvl", "wou")}
        up_in, dn_in = ([sem(f"{k}_in{i}") for i in range(2)] for k in ("up", "dn"))
        w_centred, w_hi, w_lo, wg_ready = map(sem, ("w_centred", "w_hi", "w_lo", "wg_ready"))
        up_hi, up_lo, dn_hi, dn_lo = map(sem, ("up_hi", "up_lo", "dn_hi", "dn_lo"))
        ident_zero, ident_ready, halo_zero = sem("ident_zero"), sem("ident_ready"), sem("halo_zero")
        s_dve, s_act, s_pool = sem("s_dve"), sem("s_act"), sem("s_pool")
        ln0_ready, hn_ready, ht_psum, ht_ready, ht_hi, ht_lo = map(
            sem, ("ln0_ready", "hn_ready", "ht_psum", "ht_ready", "ht_hi", "ht_lo"))
        conv_done, conv_hi, conv_lo = map(sem, ("conv_done", "conv_hi", "conv_lo"))
        qkv_psum, qkv_copied, sq_ready, ss_done, v_scaled = map(
            sem, ("qkv_psum", "qkv_copied", "sq_ready", "ss_done", "v_scaled"))
        gate_psum, gate_ready = sem("gate_psum"), sem("gate_ready")
        rr_ready, u_ready, g_ready, ut_psum, mem_ready, mem_psum = map(
            sem, ("rr_ready", "u_ready", "g_ready", "ut_psum", "mem_ready", "mem_psum"))
        centred, msq_ready, og_ready, og_psum, og_affine, o_ready, o_hi, o_lo = map(
            sem, ("centred", "msq_ready", "og_ready", "og_psum", "og_affine", "o_ready", "o_hi", "o_lo"))
        y0_ready, wo_psum, hr_ready, ln2_stats, hn2_ready, h2_psum, h2_hi, h2_lo = map(
            sem, ("y0_ready", "wo_psum", "hr_ready", "ln2_stats", "hn2_ready", "h2_psum", "h2_hi", "h2_lo"))
        up_psum, silu_ready, hid_ready, hid_hi, hid_lo, down_psum = map(
            sem, ("up_psum", "silu_ready", "hid_ready", "hid_hi", "hid_lo", "down_psum"))
        x2_stats, xn_ready, xt_psum, xt_hi, xt_lo, rt_psum, rt_copied = map(
            sem, ("x2_stats", "xn_ready", "xt_psum", "xt_hi", "xt_lo", "rt_psum", "rt_copied"))
        lmax_ready, exp_ready, pad_zero = map(sem, ("lmax_ready", "exp_ready", "pad_zero"))
        eup_psum, esilu_ready, ehid_ready, eht_psum, eht_hi, eht_lo, edown_psum, eacc_done = map(
            sem, ("eup_psum", "esilu_ready", "ehid_ready", "eht_psum", "eht_hi", "eht_lo", "edown_psum", "eacc_done"))
        out_ready = sem("out_ready")

        def f32(ap):
            return ap.bitcast(F32)

        def heads(ap):
            return ap.rearrange("p j (h d) -> p j h d", d=HD)

        def per_head(ap):
            return ap.unsqueeze(3).broadcast_to([P, J, HEADS, HD])

        def per_dim(i):
            return hvec[:, i, :].unsqueeze(1).unsqueeze(1).broadcast_to([P, J, HEADS, HD])

        def v(c, i):
            return vec[:, c, i:i + 1]

        resident = [("qkv", slice(0, 2 * D), "qkv", 32), ("qkv", slice(2 * D, 3 * D), "v", 16), ("gw", slice(0, 2 * D), "gw", 32),
                    ("wo", slice(0, D), "wo", 16), ("wgt", slice(0, FF), "wgt", 16), ("wvl", slice(0, FF), "wvl", 16),
                    ("wou", slice(0, D), "wou", 16)]
        W_QKV, W_GATES, W_O, W_UP, W_OUT = 2, 3, 4, 6, 7

        block = ctx.enter_context(nc.Block())

        @block.sync
        def _(sp):
            def rows(w):
                return w.rearrange("(c p) n -> p c n", p=P)

            def load_x(b):
                sp.dma_start(X[:, b % 2, :, :],
                             x[b * TB:(b + 1) * TB, :].rearrange("(j p) d -> p j d", p=P)).then_inc(x_in[b % 2], 16)

            def load_up(g):
                if g >= 2:
                    sp.wait_ge(eup_psum, J * (g - 1))
                sp.dma_start(raw["up"][:, g % 2], up[g % PAIRS]).then_inc(up_in[g % 2], 16)

            def load_dn(g):
                if g >= 2:
                    sp.wait_ge(edown_psum, J * (g - 1))
                d = down[g % PAIRS]
                sp.dma_start(raw["dn"][:, g % 2, 0:PK - 1, :],
                             d[0:(PK - 1) * P, :].rearrange("(k p) n -> p k n", p=P)).then_inc(dn_in[g % 2], 16)
                sp.dma_start(raw["dn"][0:LASTK, g % 2, PK - 1, :], d[(PK - 1) * P:PW, :]).then_inc(dn_in[g % 2], 16)

            def store(b):
                sp.wait_ge(out_ready, J * (b + 1))
                sp.dma_start(out[b * TB:(b + 1) * TB, :].rearrange("(j p) d -> p j d", p=P), X[:, b % 2, :, :]).then_inc(stored, 16)
                sp.wait_ge(stored, 16 * (b + 1))

            load_x(0)
            sp.dma_start(raw["qkv"][:, :, 2 * D:3 * D], rows(wv)).then_inc(w_in["v"], 16)
            sp.dma_start(raw["qkv"][:, :, 0:D], rows(wq)).then_inc(w_in["qkv"], 16)
            sp.dma_start(raw["qkv"][:, :, D:2 * D], rows(wk)).then_inc(w_in["qkv"], 16)
            sp.dma_start(vec[:, :, :], vecs).then_inc(const_in, 16)
            sp.dma_start(hvec[:, :, :], headvecs).then_inc(const_in, 16)
            sp.dma_start(wg16[:, :, :], rows(wg)).then_inc(const_in, 16)
            sp.dma_start(wr[:, :, :], router).then_inc(const_in, 16)
            sp.dma_start(raw["gw"][:, :, 0:D], rows(wig)).then_inc(w_in["gw"], 16)
            sp.dma_start(raw["gw"][:, :, D:2 * D], rows(wog)).then_inc(w_in["gw"], 16)
            sp.dma_start(raw["wo"][:, :, :], rows(wo)).then_inc(w_in["wo"], 16)
            sp.dma_start(raw["wgt"][:, :, :], rows(wgate)).then_inc(w_in["wgt"], 16)
            sp.dma_start(raw["wvl"][:, :, :], rows(wval)).then_inc(w_in["wvl"], 16)
            sp.dma_start(raw["wou"][:, :, :], rows(wout)).then_inc(w_in["wou"], 16)
            load_x(1)
            G = NB * PAIRS
            for g in range(G):
                load_up(g)
                load_dn(g)
                if g % PAIRS == 1 and g > PAIRS:
                    store(g // PAIRS - 1)
                    if g // PAIRS + 1 < NB:
                        load_x(g // PAIRS + 1)
            store(NB - 1)

        @block.gpsimd
        def _(pool):
            n_pool = [0]

            def link(ins):
                n_pool[0] += 1
                ins.then_inc(s_pool, 1)
                pool.wait_ge(s_pool, n_pool[0])

            nc.gpsimd.memset(ident[:, :], 0.0).then_inc(ident_zero, 1)
            pool.wait_ge(ident_zero, 1)
            nc.gpsimd.affine_select(out=ident[:, :], in_=ident[:, :], compare_op=ALU.not_equal, fill=1.0, base=0,
                                    pattern=[[-1, P]], channel_multiplier=1).then_inc(ident_ready, 1)

            def split(i):
                k, cols, _, _ = resident[i]
                pool.wait_ge(w_hi, i + 1)
                nc.gpsimd.tensor_tensor(lo[k][:, :, cols], raw[k][:, :, cols], f32(hi[k][:, :, cols]),
                                        ALU.subtract).then_inc(w_lo, 1)

            def split_up(g):
                pool.wait_ge(up_hi, g + 1)
                nc.gpsimd.tensor_tensor(lo["up"][:, g % 2], raw["up"][:, g % 2], f32(hi["up"][:, g % 2]),
                                        ALU.subtract).then_inc(up_lo, 1)

            def split_dn(g):
                pool.wait_ge(dn_hi, 2 * (g + 1))
                for rws, ks in ((slice(0, P), slice(0, PK - 1)), (slice(0, LASTK), slice(PK - 1, PK))):
                    nc.gpsimd.tensor_tensor(lo["dn"][rws, g % 2, ks], raw["dn"][rws, g % 2, ks],
                                            f32(hi["dn"][rws, g % 2, ks]), ALU.subtract).then_inc(dn_lo, 1)

            split(0)
            split(1)

            def at(stage, b, m):
                if (stage, m) == ("ht", 1):
                    for c in range(C):
                        pool.wait_ge(ht_hi, C * b + c + 1)
                        nc.gpsimd.tensor_tensor(AL[:, c, :], HT[:, c, KC - 1:], f32(AH[:, c, :]),
                                                ALU.subtract).then_inc(ht_lo, 1)
                    if b == 0:
                        split(2)
                        split(3)
                if stage == "q":
                    pool.wait_ge(sq_ready, J * b + m + 1)
                    vj = QKV[:, m, 2 * D:3 * D].rearrange("p (h d) -> p h d", d=HD)
                    nc.gpsimd.tensor_tensor(vj, vj, hvec[:, 0, :].unsqueeze(1).broadcast_to([P, HEADS, HD]),
                                            ALU.mult).then_inc(v_scaled, 1)
                if (stage, m) == ("xs", 1):
                    for c in range(C):
                        pool.wait_ge(conv_hi, C * b + c + 1)
                        nc.gpsimd.tensor_tensor(AL[:, c, :], XC[:, c, :], f32(AH[:, c, :]),
                                                ALU.subtract).then_inc(conv_lo, 1)
                    if b == 0:
                        for i in range(4, 7):
                            split(i)
                        for g in range(2):
                            split_up(g)
                            split_dn(g)
                if stage == "scan":
                    q, k, w = (heads(QKV[:, :, i * D:(i + 1) * D]) for i in range(3))
                    if m == 0:
                        pool.wait_ge(rr_ready, b + 1)
                        link(nc.gpsimd.tensor_tensor(q, q, per_head(rr[:, :, 0:HEADS]), ALU.mult))
                        pool.wait_ge(u_ready, b + 1)
                        nc.gpsimd.tensor_tensor(k, q, per_dim(2), ALU.mult).then_inc(g_ready, 1)
                    else:
                        pool.wait_ge(ut_psum, b + 1)
                        nc.gpsimd.tensor_tensor(w, q, per_dim(3), ALU.mult).then_inc(g_ready, 1)
                if stage == "mup":
                    n = FM * b + m
                    pool.wait_ge(hid_hi, n + 1)
                    nc.gpsimd.tensor_tensor(HML[:, n % 2, :], SM[:, n % 2, :], f32(HMH[:, n % 2, :]),
                                            ALU.subtract).then_inc(hid_lo, 1)
                if stage == "refill_up" and b * PAIRS + m < NB * PAIRS:
                    split_up(b * PAIRS + m)
                if stage == "refill_dn" and b * PAIRS + m < NB * PAIRS:
                    split_dn(b * PAIRS + m)

            for name, b, m in steps("pool"):
                at(name, b, m)

        @block.scalar
        def _(act):
            n_act = [0]

            def step(ins):
                n_act[0] += 1
                ins.then_inc(s_act, 1)

            def settle():
                act.wait_ge(s_act, n_act[0])

            def split(i):
                k, cols, arrival, count = resident[i]
                act.wait_ge(w_in[arrival], count)
                if arrival == "v":
                    act.wait_ge(w_centred, 1)
                nc.scalar.activation(hi[k][:, :, cols], raw[k][:, :, cols], ACT.Copy).then_inc(w_hi, 1)

            def split_up(g):
                act.wait_ge(up_in[g % 2], 16 * (g // 2 + 1))
                nc.scalar.activation(hi["up"][:, g % 2], raw["up"][:, g % 2], ACT.Copy).then_inc(up_hi, 1)

            def split_dn(g):
                act.wait_ge(dn_in[g % 2], 32 * (g // 2 + 1))
                for rws, ks in ((slice(0, P), slice(0, PK - 1)), (slice(0, LASTK), slice(PK - 1, PK))):
                    nc.scalar.activation(hi["dn"][rws, g % 2, ks], raw["dn"][rws, g % 2, ks], ACT.Copy).then_inc(dn_hi, 1)

            split(0)

            def at(stage, b, m):
                if (stage, m) == ("ln0", 2):
                    act.wait_ge(ln0_ready, b + 1)
                    if b > 0:
                        act.wait_ge(h2_psum, b)
                    for j in range(J):
                        nc.scalar.activation(HN[:, j, :], X[:, b % 2, j, :], ACT.Identity, bias=n1[:, j:j + 1],
                                             scale=s1[:, j:j + 1]).then_inc(hn_ready, 1)
                    if b == 0:
                        split(1)
                if (stage, m) == ("ht", 0):
                    if b == 0:
                        act.wait_ge(const_in, 64)
                        act.wait_ge(halo_zero, 1)
                    else:
                        act.wait_ge(conv_done, C * b)
                        act.wait_ge(ht_lo, C * b)
                        step(nc.scalar.activation(HT[:, :, 0:KC - 1], HT[:, :, TB:TB + KC - 1], ACT.Copy))
                        settle()
                    act.wait_ge(ht_psum, b + 1)
                    for c in range(C):
                        nc.scalar.activation(HT[:, c, KC - 1:], p_main[:, c, :], ACT.Identity, bias=v(c, LN1B),
                                             scale=v(c, LN1W)).then_inc(ht_ready, 1)
                if (stage, m) == ("ht", 1):
                    if b > 0:
                        act.wait_ge(wo_psum, b)
                    for c in range(C):
                        act.wait_ge(ht_ready, C * b + c + 1)
                        nc.scalar.activation(AH[:, c, :], HT[:, c, KC - 1:], ACT.Copy).then_inc(ht_hi, 1)
                    if b == 0:
                        split(2)
                        split(3)
                if stage == "q":
                    n = J * b + m
                    act.wait_ge(qkv_psum, n + 1)
                    nc.scalar.activation(QKV[:, m, :], p_main.rearrange("p a n -> p (a n)")[:, 0:3 * D],
                                         ACT.Copy).then_inc(qkv_copied, 1)
                    act.wait_ge(qkv_copied, n + 1)
                    if n >= 2:
                        act.wait_ge(ss_done, n - 1)
                    nc.scalar.activation(SQ[n % 2], QKV[:, m, :], ACT.Square).then_inc(sq_ready, 1)
                if (stage, m) == ("xs", 0):
                    for c in range(C):
                        act.wait_ge(conv_done, C * b + c + 1)
                        step(nc.scalar.activation(XC[:, c, :], XC[:, c, :], ACT.Silu))
                if (stage, m) == ("xs", 1):
                    settle()
                    act.wait_ge(qkv_psum, J * (b + 1))
                    for c in range(C):
                        nc.scalar.activation(AH[:, c, :], XC[:, c, :], ACT.Copy).then_inc(conv_hi, 1)
                    if b == 0:
                        for i in range(4, 7):
                            split(i)
                        for g in range(2):
                            split_up(g)
                            split_dn(g)
                if stage == "g":
                    dst, bias = ((IG, BIG), (OG, BOG), (GA, BG))[m]
                    act.wait_ge(gate_psum, 3 * b + m + 1)
                    if m == 0:
                        act.wait_ge(ss_done, J * (b + 1))
                        if b > 0:
                            act.wait_ge(h2_lo, C * b)
                    for c in range(C):
                        nc.scalar.activation(dst[:, c, :], p_main[:, c, :], ACT.Sigmoid,
                                             bias=v(c, bias)).then_inc(gate_ready, 1)
                if stage == "centre":
                    act.wait_ge(centred, 2 * b + m + 1)
                    nc.scalar.activation(MSQ, HN[:, :, :].rearrange("p j d -> p (j d)"), ACT.Square).then_inc(msq_ready, 1)
                if (stage, m) == ("og", 0):
                    act.wait_ge(og_psum, b + 1)
                    for c in range(C):
                        nc.scalar.activation(GA[:, c, :], p_main[:, c, :], ACT.Identity, bias=v(c, GNB),
                                             scale=v(c, GNW)).then_inc(og_affine, 1)
                if (stage, m) == ("o", 0):
                    for c in range(C):
                        act.wait_ge(o_ready, C * b + c + 1)
                        nc.scalar.activation(AH[:, c, :], OG[:, c, :], ACT.Copy).then_inc(o_hi, 1)
                if stage == "y0":
                    act.wait_ge(og_psum, b + 1)
                    for j in range(J):
                        nc.scalar.activation(HN[:, j, :], X[:, b % 2, j, :], ACT.Identity, bias=n0[:, j:j + 1],
                                             scale=r0[:, j:j + 1]).then_inc(y0_ready, 1)
                if (stage, m) == ("ln2", 1):
                    act.wait_ge(ln2_stats, b + 1)
                    for j in range(J):
                        nc.scalar.activation(HN[:, j, :], HR[:, j, :], ACT.Identity, bias=l2n[:, j:j + 1],
                                             scale=l2r[:, j:j + 1]).then_inc(hn2_ready, 1)
                if (stage, m) == ("h2", 0):
                    act.wait_ge(h2_psum, b + 1)
                    for c in range(C):
                        step(nc.scalar.activation(GA[:, c, :], p_main[:, c, :], ACT.Identity, bias=v(c, LN2B),
                                                  scale=v(c, LN2W)))
                if (stage, m) == ("h2", 1):
                    settle()
                    if b > 0:
                        act.wait_ge(up_psum, FM * b)
                    for c in range(C):
                        nc.scalar.activation(H2H[:, c, :], GA[:, c, :], ACT.Copy).then_inc(h2_hi, 1)
                if stage == "mup":
                    n = FM * b + m
                    act.wait_ge(up_psum, n + 1)
                    if n >= 2:
                        act.wait_ge(down_psum, n - 1)
                    nc.scalar.activation(SM[:, n % 2, :], p_pair(n)[0], ACT.Silu).then_inc(silu_ready, 1)
                    act.wait_ge(hid_ready, n + 1)
                    nc.scalar.activation(HMH[:, n % 2, :], SM[:, n % 2, :], ACT.Copy).then_inc(hid_hi, 1)
                if (stage, m) == ("x2", 1):
                    act.wait_ge(x2_stats, b + 1)
                    for j in range(J):
                        nc.scalar.activation(HR[:, j, :], X[:, b % 2, j, :], ACT.Identity, bias=x2n[:, j:j + 1],
                                             scale=x2r[:, j:j + 1]).then_inc(xn_ready, 1)
                if stage == "xt":
                    act.wait_ge(xt_psum, b + 1)
                    for c in range(C):
                        nc.scalar.activation(XTH[:, c, :], p_down[:, c, :], ACT.Copy).then_inc(xt_hi, 1)
                if (stage, m) == ("choose", 0):
                    act.wait_ge(lmax_ready, b + 1)
                    nc.scalar.activation(ex[:, :, :], ex[:, :, :], ACT.Exp).then_inc(exp_ready, 1)
                if stage == "up":
                    n = UNITS * b + m
                    act.wait_ge(eup_psum, n + 1)
                    if n >= 2:
                        act.wait_ge(eht_psum, n - 1)
                    nc.scalar.activation(hb[:, n % 2, 0:PW], p_pair(n)[0][:, 0:PW], ACT.Silu).then_inc(esilu_ready, 1)
                if stage == "turn":
                    n = UNITS * b + m
                    act.wait_ge(eht_psum, n + 1)
                    if n >= 2:
                        act.wait_ge(edown_psum, n - 1)
                    nc.scalar.activation(htH[:, n % 2, :], p_turn, ACT.Copy).then_inc(eht_hi, 1)
                if stage == "refill_up" and b * PAIRS + m < NB * PAIRS:
                    split_up(b * PAIRS + m)
                if stage == "refill_dn" and b * PAIRS + m < NB * PAIRS:
                    split_dn(b * PAIRS + m)

            for name, b, m in steps("act"):
                at(name, b, m)

        @block.tensor
        def _(pe):
            def mm3(dst, aH, aL, bH, bL, start, stop, shared=False):
                nc.tensor.matmul(dst, aH, bH, start=start, stop=False, skip_group_check=shared)
                nc.tensor.matmul(dst, aH, bL, start=False, stop=False, skip_group_check=shared)
                return nc.tensor.matmul(dst, aL, bH, start=False, stop=stop, skip_group_check=shared)

            def to_features(dst, src):
                for c in range(C):
                    for j in range(J):
                        last = nc.tensor.transpose(dst[:, c, j * P:(j + 1) * P], src(j)[:, c * P:(c + 1) * P], ident[:, :])
                return last

            pe.wait_ge(ident_ready, 1)

            def mlp_up(n):
                m = n % FM
                if m == 0 and n > 0:
                    pe.wait_ge(ehid_ready, 2 * UNITS * (n // FM))
                if n >= 2:
                    pe.wait_ge(hid_ready, n - 1)
                for dst, w in zip(p_pair(n), ("wgt", "wvl")):
                    for c in range(C):
                        cols = slice(m * P, (m + 1) * P)
                        last = mm3(dst, hi[w][:, c, cols], lo[w][:, c, cols], H2H[:, c, :], H2L[:, c, :], c == 0, c == C - 1)
                last.then_inc(up_psum, 1)

            def mlp_down(n):
                m = n % FM
                pe.wait_ge(hid_lo, n + 1)
                for j in range(J):
                    cols = slice(j * P, (j + 1) * P)
                    last = mm3(p_down[:, j // 2, (j % 2) * D:(j % 2 + 1) * D], HMH[:, n % 2, cols], HML[:, n % 2, cols],
                               hi["wou"][:, m, :], lo["wou"][:, m, :], m == 0 and j % 2 == 0, m == FM - 1, shared=True)
                last.then_inc(down_psum, 1)

            def up_product(b, k):
                n, i = UNITS * b + k, (k // J) % 2
                if k % J == 0:
                    pe.wait_ge(up_lo, b * PAIRS + k // J + 1)
                if k < 2:
                    pe.wait_ge(hid_ready, FM * (b + 1))
                else:
                    pe.wait_ge(ehid_ready, 2 * (n - 1))
                cols = slice((k % J) * P, (k % J + 1) * P)
                for half, dst in enumerate(p_pair(n)):
                    w = slice(half * PW, (half + 1) * PW)
                    for c in range(C):
                        last = mm3(dst[:, 0:PW], XTH[:, c, cols], XTL[:, c, cols], hi["up"][:, i, c, w],
                                   lo["up"][:, i, c, w], c == 0, c == C - 1)
                last.then_inc(eup_psum, 1)

            def down_product(b, k):
                n, i = UNITS * b + k, (k // J) % 2
                if k % J == 0:
                    pe.wait_ge(dn_lo, 2 * (b * PAIRS + k // J + 1))
                pe.wait_ge(eht_lo, n + 1)
                if n >= 1:
                    pe.wait_ge(eacc_done, n)
                for kk in range(PK):
                    rws = P if kk < PK - 1 else LASTK
                    hid = slice(kk * P, (kk + 1) * P)
                    last = mm3(p_part, htH[0:rws, n % 2, hid], htL[0:rws, n % 2, hid], hi["dn"][0:rws, i, kk, :],
                               lo["dn"][0:rws, i, kk, :], kk == 0, kk == PK - 1)
                last.then_inc(edown_psum, 1)

            def turn(b, k):
                n = UNITS * b + k
                pe.wait_ge(ehid_ready, 2 * (n + 1))
                if k == 0:
                    pe.wait_ge(rt_copied, b + 1)
                    if b == 0:
                        pe.wait_ge(pad_zero, 1)
                if n >= 1:
                    pe.wait_ge(eht_lo, n)
                for kk in range(PK):
                    last = nc.tensor.transpose(p_turn[:, kk * P:(kk + 1) * P], hb[:, n % 2, kk * P:(kk + 1) * P], ident[:, :])
                last.then_inc(eht_psum, 1)

            def at(stage, b, m):
                if (stage, m) == ("ht", 0):
                    pe.wait_ge(hn_ready, J * (b + 1))
                    to_features(p_main, lambda j: HN[:, j, :]).then_inc(ht_psum, 1)
                if stage == "q":
                    n = J * b + m
                    if m == 0:
                        if b == 0:
                            pe.wait_ge(w_lo, W_QKV)
                        pe.wait_ge(ht_lo, C * (b + 1))
                    else:
                        pe.wait_ge(qkv_copied, n)
                    tok = slice(m * P, (m + 1) * P)
                    for part, cols in ((0, slice(0, 2 * D)), (1, slice(2 * D, 3 * D))):
                        for c in range(C):
                            last = mm3(p_main[:, part, 0:cols.stop - cols.start], AH[:, c, tok], AL[:, c, tok],
                                       hi["qkv"][:, c, cols], lo["qkv"][:, c, cols], c == 0, c == C - 1)
                    last.then_inc(qkv_psum, 1)
                if stage == "g":
                    if m == 0:
                        pe.wait_ge(qkv_copied, J * (b + 1))
                        if b == 0:
                            pe.wait_ge(w_lo, W_GATES)
                            pe.wait_ge(wg_ready, 1)
                        pe.wait_ge(conv_lo, C * (b + 1))
                    else:
                        pe.wait_ge(gate_ready, C * (3 * b + m))
                    for o in range(C):
                        for c in range(C):
                            if m < 2:
                                wH, wL = (w["gw"][:, c, m * D + o * P:m * D + (o + 1) * P] for w in (hi, lo))
                                last = mm3(p_main[:, o, :], wH, wL, AH[:, c, :], AL[:, c, :], c == 0, c == C - 1)
                            else:
                                last = nc.tensor.matmul(p_main[:, o, :], wgx[:, c, o * P:(o + 1) * P], XC[:, c, :],
                                                        start=c == 0, stop=c == C - 1)
                    last.then_inc(gate_psum, 1)
                if stage == "ut":
                    pe.wait_ge(u_ready, b + 1)
                    pe.wait_ge(gate_ready, 3 * C * (b + 1))
                    to_features(p_main, lambda j: QKV[:, j, 2 * D:3 * D]).then_inc(ut_psum, 1)
                if stage == "mt":
                    pe.wait_ge(mem_ready, C * (b + 1))
                    for j in range(J):
                        for c in range(C):
                            last = nc.tensor.transpose(p_main[:, j // 2, (j % 2) * D + c * P:(j % 2) * D + (c + 1) * P],
                                                       IG[:, c, j * P:(j + 1) * P], ident[:, :])
                    last.then_inc(mem_psum, 1)
                if stage == "og":
                    pe.wait_ge(og_ready, b + 1)
                    to_features(p_main, lambda j: HN[:, j, :]).then_inc(og_psum, 1)
                if stage == "wo":
                    if b == 0:
                        pe.wait_ge(w_lo, W_O)
                    pe.wait_ge(o_lo, C * (b + 1))
                    for j in range(J):
                        cols = slice(j * P, (j + 1) * P)
                        for c in range(C):
                            last = mm3(p_main[:, j // 2, (j % 2) * D:(j % 2 + 1) * D], AH[:, c, cols], AL[:, c, cols],
                                       hi["wo"][:, c, :], lo["wo"][:, c, :], c == 0, c == C - 1)
                    last.then_inc(wo_psum, 1)
                if (stage, m) == ("h2", 0):
                    pe.wait_ge(hn2_ready, J * (b + 1))
                    to_features(p_main, lambda j: HN[:, j, :]).then_inc(h2_psum, 1)
                if stage == "mup":
                    if m == 0:
                        pe.wait_ge(h2_lo, C * (b + 1))
                        if b == 0:
                            pe.wait_ge(w_lo, W_UP)
                    mlp_up(FM * b + m)
                if stage == "mdn":
                    if m == 0:
                        if b == 0:
                            pe.wait_ge(w_lo, W_OUT)
                        else:
                            pe.wait_ge(eacc_done, UNITS * b)
                    mlp_down(FM * b + m)
                if stage == "xt":
                    pe.wait_ge(xn_ready, J * (b + 1))
                    to_features(p_down, lambda j: HR[:, j, :]).then_inc(xt_psum, 1)
                if stage == "route":
                    pe.wait_ge(xt_lo, C * (b + 1))
                    for j in range(J):
                        t = slice(j * P, (j + 1) * P)
                        for i, (a, c) in enumerate((a, c) for a in (XTH, XTL) for c in range(C)):
                            last = nc.tensor.matmul(p_turn[:, j * RW:(j + 1) * RW], f32(a[:, c, t]), wr[:, c, :],
                                                    start=i == 0, stop=i == 2 * C - 1)
                    last.then_inc(rt_psum, 1)
                if stage == "up":
                    up_product(b, m)
                if stage == "turn":
                    turn(b, m)
                if stage == "down":
                    down_product(b, m)

            for name, b, m in steps("pe"):
                at(name, b, m)

        @block.vector
        def _(dve):
            n_dve = [0]

            def step(ins):
                n_dve[0] += 1
                ins.then_inc(s_dve, 1)

            def settle():
                dve.wait_ge(s_dve, n_dve[0])

            def link(ins):
                step(ins)
                settle()

            def guess(a, y):
                link(nc.vector.tensor_scalar(y.bitcast(I32), a.bitcast(I32), 1, None, ALU.logical_shift_right))
                step(nc.vector.tensor_scalar(y.bitcast(I32), y.bitcast(I32), -1.0, float(0x5F3759DF), ALU.mult, ALU.add))

            def newton(a, y, t, out):
                settle()
                link(nc.vector.tensor_tensor(t, y, y, ALU.mult))
                link(nc.vector.scalar_tensor_tensor(t, t, -0.5, a, ALU.mult, ALU.mult))
                return nc.vector.scalar_tensor_tensor(out, t, 1.5, y, ALU.add, ALU.mult)

            def rsqrt(out, a, y, t):
                guess(a, y)
                for i in range(2):
                    step(newton(a, y, t, y))
                return newton(a, y, t, out)

            def scratch(n):
                return va[:, 0:n], rs[:, 0:n], rt[:, 0:n]

            MINE, EXPERTS_OWN = (st, mv, va[:, 0:J]), (est, emv, eva[:, :])

            def stats(tile, own):
                s, m, a = own
                for j in range(J):
                    step(nc.vector.bn_stats(s[:, j, :], tile(j)))
                settle()
                for j in range(J):
                    step(nc.vector.bn_aggr(m[:, j, :], s[:, j, :]))
                settle()
                link(nc.vector.tensor_scalar(a, m[:, :, 1], EPS, None, ALU.add))

            def minus_mean(dst, scale, means):
                return nc.vector.scalar_tensor_tensor(dst[:, :], means[:, :, 0], -1.0, scale[:, :], ALU.mult, ALU.mult)

            step(nc.vector.memset(carry[:, :], 0.0))
            nc.vector.memset(HT[:, :, 0:KC - 1], 0.0).then_inc(halo_zero, 1)
            nc.vector.memset(hb[:, :, PW:PK * P], 0.0).then_inc(pad_zero, 1)
            for e in range(E):
                step(nc.vector.memset(rank[:, e:e + 1], float(E - e)))
            settle()

            def prepare_weights():
                dve.wait_ge(w_in["v"], 16)
                wv_raw = raw["qkv"][:, :, 2 * D:3 * D].rearrange("p c (h d) -> p c h d", d=HD)
                link(nc.vector.tensor_reduce(wmean[:, :, :], wv_raw, AX_X, ALU.add))
                link(nc.vector.tensor_scalar(wmean[:, :, :], wmean[:, :, :], -1.0 / HD, None, ALU.mult))
                nc.vector.tensor_tensor(wv_raw, wv_raw, wmean[:, :, :].unsqueeze(3).broadcast_to([P, C, HEADS, HD]),
                                        ALU.add).then_inc(w_centred, 1)
                dve.wait_ge(const_in, 64)
                nc.vector.tensor_copy(wgx[:, :, :].rearrange("p c (h d) -> p c h d", d=HD),
                                      wg16[:, :, :].unsqueeze(3).broadcast_to([P, C, HEADS, HD])).then_inc(wg_ready, 1)

            def flat(ap):
                return ap.rearrange("p j d -> p (j d)")

            def by_head(ap):
                return ap.rearrange("p (h d) -> p h d", d=HD)

            G = J * HEADS
            m_flat = by_head(flat(HN[:, :, :]))

            def spread(ap):
                return ap.unsqueeze(2).broadcast_to([P, G, HD])

            def wide(ap):
                return ap.unsqueeze(2).broadcast_to([P, J, E])

            e8 = ex[:, :, 0:E]
            ranks = rank[:, :].unsqueeze(1).broadcast_to([P, J, E])

            def choose(i):
                src = e8 if i == 0 else key[:, :, :]
                link(nc.vector.tensor_reduce(top[:, 1, :], src, AX_X, ALU.max))
                link(nc.vector.tensor_tensor(pick[:, i], src, wide(top[:, 1, :]), ALU.is_equal))
                link(nc.vector.tensor_tensor(pick[:, i], pick[:, i], ranks, ALU.mult))
                link(nc.vector.tensor_reduce(top[:, 2, :], pick[:, i], AX_X, ALU.max))
                link(nc.vector.tensor_tensor(pick[:, i], pick[:, i], wide(top[:, 2, :]), ALU.is_equal))
                if i == 0:
                    step(nc.vector.scalar_tensor_tensor(key[:, :, :], pick[:, 0], -2.0, e8, ALU.mult, ALU.add))

            def weigh():
                step(nc.vector.tensor_tensor(pick[:, 0], pick[:, 0], pick[:, 1], ALU.add))
                link(nc.vector.tensor_scalar(top[:, 2, :], ex[:, :, E], 1.0, None, ALU.add))
                step(nc.vector.tensor_tensor(key[:, :, :], e8, pick[:, 0], ALU.mult))
                link(nc.vector.reciprocal(top[:, 1, :], top[:, 2, :]))
                step(nc.vector.tensor_reduce(top[:, 3, :], key[:, :, :], AX_X, ALU.add))
                link(nc.vector.tensor_copy(cw[:, :, E:NE], top[:, 1, :].unsqueeze(2).broadcast_to([P, J, SL])))
                link(nc.vector.reciprocal(top[:, 3, :], top[:, 3, :]))
                step(nc.vector.tensor_tensor(cw[:, :, 0:E], key[:, :, :], wide(top[:, 3, :]), ALU.mult))

            def at(stage, b, m):
                xb = X[:, b % 2]
                if stage == "ln0":
                    if m == 0:
                        dve.wait_ge(x_in[b % 2], 16 * (b // 2 + 1))
                        stats(lambda j: xb[:, j, :], MINE)
                    if m == 1:
                        if b > 0:
                            dve.wait_ge(y0_ready, J * b)
                        link(rsqrt(r0[:, :], *scratch(J)))
                        step(minus_mean(n0, r0, mv))
                        link(nc.vector.tensor_tensor(va[:, 0:J], mv[:, :, 1], r0[:, :], ALU.mult))
                        link(nc.vector.tensor_tensor(va[:, 0:J], va[:, 0:J], r0[:, :], ALU.mult))
                        step(nc.vector.tensor_scalar(va[:, 0:J], va[:, 0:J], EPS, None, ALU.add))
                    if m == 2:
                        settle()
                        link(rsqrt(rs[:, 0:J], *scratch(J)))
                        link(nc.vector.tensor_tensor(s1[:, :], r0[:, :], rs[:, 0:J], ALU.mult))
                        minus_mean(n1, s1, mv).then_inc(ln0_ready, 1)
                        if b == 0:
                            prepare_weights()
                if stage == "conv":
                    if m == 0:
                        if b > 0:
                            dve.wait_ge(conv_lo, C * b)
                            dve.wait_ge(gate_psum, 3 * b)
                        for c in range(C):
                            dve.wait_ge(ht_ready, C * b + c + 1)
                            step(nc.vector.tensor_scalar(XC[:, c, :], HT[:, c, 0:TB], v(c, CONVW), v(c, CONVB), ALU.mult,
                                                         ALU.add))
                    else:
                        settle()
                        for c in range(C):
                            ins = nc.vector.scalar_tensor_tensor(XC[:, c, :], HT[:, c, m:m + TB], v(c, CONVW + m),
                                                                 XC[:, c, :], ALU.mult, ALU.add)
                            if m < KC - 1:
                                step(ins)
                            else:
                                ins.then_inc(conv_done, 1)
                if stage == "q":
                    n = J * b + m
                    dve.wait_ge(sq_ready, n + 1)
                    if b > 0 and m == 0:
                        dve.wait_ge(g_ready, 2 * b)
                    nc.vector.tensor_reduce(rr[:, m, :], by_head(SQ[n % 2]), AX_X,
                                            ALU.add).then_inc(ss_done, 1)
                if stage == "rs":
                    a, y, t = scratch(J * 3 * HEADS)
                    if m == 0:
                        dve.wait_ge(ss_done, J * (b + 1))
                        args = va[:, :].rearrange("p (j h) -> p j h", j=J)
                        step(nc.vector.tensor_scalar(args[:, :, 0:2 * HEADS], rr[:, :, 0:2 * HEADS], 1e-12, None, ALU.add))
                        link(nc.vector.tensor_scalar(args[:, :, 2 * HEADS:], rr[:, :, 2 * HEADS:], 1.0 / HD, EPS,
                                                     ALU.mult, ALU.add))
                        guess(a, y)
                        step(newton(a, y, t, y))
                    else:
                        step(newton(a, y, t, y))
                        newton(a, y, t, rr[:, :, :].rearrange("p j h -> p (j h)")).then_inc(rr_ready, 1)
                if stage == "u":
                    k, w = heads(QKV[:, :, D:2 * D]), heads(QKV[:, :, 2 * D:3 * D])
                    settle()
                    if m == 0:
                        dve.wait_ge(rr_ready, b + 1)
                        dve.wait_ge(v_scaled, J * (b + 1))
                        step(nc.vector.tensor_tensor(w, w, per_head(rr[:, :, 2 * HEADS:]), ALU.mult))
                    if m == 1:
                        step(nc.vector.tensor_tensor(k, k, per_head(rr[:, :, HEADS:2 * HEADS]), ALU.mult))
                    if m == 2:
                        step(nc.vector.tensor_tensor(w, w, per_dim(1), ALU.add))
                    if m == 3:
                        nc.vector.tensor_tensor(w, w, k, ALU.mult).then_inc(u_ready, 1)
                if (stage, m) == ("scan", 0):
                    dve.wait_ge(gate_ready, 3 * C * (b + 1))
                    dve.wait_ge(ut_psum, b + 1)
                    for c in range(C):
                        step(nc.vector.tensor_tensor(IG[:, c, :], IG[:, c, :], p_main[:, c, :], ALU.mult))
                if (stage, m) == ("scan", 1):
                    settle()
                    for c in range(C):
                        nc.vector.tensor_tensor_scan(IG[:, c, :], GA[:, c, :], IG[:, c, :], carry[:, c:c + 1], ALU.mult,
                                                     ALU.add).then_inc(mem_ready, 1)
                    dve.wait_ge(mem_ready, C * (b + 1))
                    step(nc.vector.tensor_copy(carry[:, :], IG[:, :, TB - 1]))
                if stage == "mean":
                    if m == 0:
                        dve.wait_ge(mem_psum, b + 1)
                    settle()
                    src = flat(p_main) if m == 0 else flat(HN[:, :, :])
                    link(nc.vector.tensor_reduce(mu[:, :], by_head(src), AX_X, ALU.add))
                    step(nc.vector.tensor_scalar(mu[:, :], mu[:, :], -1.0 / HD, None, ALU.mult))
                if stage == "centre":
                    settle()
                    src = flat(p_main) if m == 0 else flat(HN[:, :, :])
                    nc.vector.tensor_tensor(m_flat, by_head(src), spread(mu[:, :]), ALU.add).then_inc(centred, 1)
                if stage == "var":
                    dve.wait_ge(msq_ready, 2 * b + m + 1)
                    link(nc.vector.tensor_reduce(va[:, 0:G], by_head(MSQ), AX_X, ALU.add))
                    step(nc.vector.tensor_scalar(va[:, 0:G], va[:, 0:G], 1.0 / HD, EPS, ALU.mult, ALU.add))
                if stage == "rstd":
                    settle()
                    step(rsqrt(mu[:, :], *scratch(G)))
                if stage == "norm":
                    settle()
                    ins = nc.vector.tensor_tensor(m_flat, m_flat, spread(mu[:, :]), ALU.mult)
                    if m == 0:
                        step(ins)
                    else:
                        ins.then_inc(og_ready, 1)
                if stage == "affine":
                    settle()
                    if m == 0:
                        dve.wait_ge(g_ready, 2 * (b + 1))
                        step(nc.vector.tensor_tensor(HN[:, :, :], HN[:, :, :], QKV[:, :, D:2 * D], ALU.mult))
                    else:
                        step(nc.vector.tensor_tensor(HN[:, :, :], HN[:, :, :], QKV[:, :, 2 * D:], ALU.add))
                if (stage, m) == ("o", 0):
                    for c in range(C):
                        dve.wait_ge(og_affine, C * b + c + 1)
                        nc.vector.tensor_tensor(OG[:, c, :], OG[:, c, :], GA[:, c, :], ALU.mult).then_inc(o_ready, 1)
                if (stage, m) == ("o", 1):
                    for c in range(C):
                        dve.wait_ge(o_hi, C * b + c + 1)
                        nc.vector.tensor_tensor(AL[:, c, :], OG[:, c, :], f32(AH[:, c, :]), ALU.subtract).then_inc(o_lo, 1)
                if stage == "wo":
                    dve.wait_ge(wo_psum, b + 1)
                    dve.wait_ge(y0_ready, J * (b + 1))
                    if b > 0:
                        dve.wait_ge(xt_psum, b)
                    nc.vector.tensor_tensor(flat(HR[:, :, :]), flat(p_main), flat(HN[:, :, :]), ALU.add).then_inc(hr_ready, 1)
                if (stage, m) == ("ln2", 0):
                    dve.wait_ge(hr_ready, b + 1)
                    stats(lambda j: HR[:, j, :], MINE)
                if (stage, m) == ("ln2", 1):
                    link(rsqrt(l2r[:, :], *scratch(J)))
                    minus_mean(l2n, l2r, mv).then_inc(ln2_stats, 1)
                if (stage, m) == ("h2", 1):
                    for c in range(C):
                        dve.wait_ge(h2_hi, C * b + c + 1)
                        nc.vector.tensor_tensor(H2L[:, c, :], GA[:, c, :], f32(H2H[:, c, :]), ALU.subtract).then_inc(h2_lo, 1)
                if stage == "mup":
                    n = FM * b + m
                    dve.wait_ge(silu_ready, n + 1)
                    nc.vector.tensor_tensor(SM[:, n % 2, :], SM[:, n % 2, :], p_pair(n)[1], ALU.mult).then_inc(hid_ready, 1)
                if (stage, m) == ("sum", 0):
                    dve.wait_ge(down_psum, FM * (b + 1))
                    link(nc.vector.tensor_tensor(flat(HR[:, :, :]), flat(HR[:, :, :]), flat(p_down), ALU.add))
                    stats(lambda j: HR[:, j, :], EXPERTS_OWN)
                if (stage, m) == ("sum", 1):
                    link(rsqrt(ers[:, :], eva[:, :], ers[:, :], ert[:, :]))
                    for j in range(J):
                        step(nc.vector.tensor_scalar(HR[:, j, :], HR[:, j, :], emv[:, j, 0:1], ers[:, j:j + 1],
                                                     ALU.subtract, ALU.mult))
                    settle()
                    step(nc.vector.tensor_tensor(xb, xb, HR[:, :, :], ALU.add))
                if (stage, m) == ("x2", 0):
                    settle()
                    stats(lambda j: xb[:, j, :], EXPERTS_OWN)
                if (stage, m) == ("x2", 1):
                    link(rsqrt(x2r[:, :], eva[:, :], ers[:, :], ert[:, :]))
                    minus_mean(x2n, x2r, emv).then_inc(x2_stats, 1)
                if stage == "xt":
                    for c in range(C):
                        dve.wait_ge(xt_hi, C * b + c + 1)
                        nc.vector.tensor_tensor(XTL[:, c, :], p_down[:, c, :], f32(XTH[:, c, :]), ALU.subtract).then_inc(xt_lo, 1)
                if stage == "route":
                    dve.wait_ge(rt_psum, b + 1)
                    nc.vector.tensor_copy(LG[:, :, :], p_turn[:, 0:J * RW].rearrange("p (j r) -> p j r", r=RW)).then_inc(rt_copied, 1)
                if (stage, m) == ("choose", 0):
                    dve.wait_ge(rt_copied, b + 1)
                    step(nc.vector.tensor_reduce(top[:, 0, :], LG[:, :, 0:E], AX_X, ALU.max))
                    step(nc.vector.tensor_scalar(ex[:, :, E], LG[:, :, E], -1.0, None, ALU.mult))
                    settle()
                    nc.vector.tensor_tensor(ex[:, :, 0:E], LG[:, :, 0:E], wide(top[:, 0, :]), ALU.subtract).then_inc(lmax_ready, 1)
                if (stage, m) == ("choose", 1):
                    dve.wait_ge(exp_ready, b + 1)
                    choose(0)
                if (stage, m) == ("choose", 2):
                    settle()
                    choose(1)
                if (stage, m) == ("choose", 3):
                    weigh()
                if stage == "up":
                    n, p, t = UNITS * b + m, m // J, m % J
                    if m == 0:
                        settle()
                    dve.wait_ge(esilu_ready, n + 1)
                    for e in range(2):
                        cols = slice(e * EI, (e + 1) * EI)
                        nc.vector.scalar_tensor_tensor(hb[:, n % 2, cols], hb[:, n % 2, cols],
                                                       cw[:, t, 2 * p + e:2 * p + e + 1], p_pair(n)[1][:, cols],
                                                       ALU.mult, ALU.mult).then_inc(ehid_ready, 1)
                if stage == "turn":
                    n = UNITS * b + m
                    dve.wait_ge(eht_hi, n + 1)
                    if n >= 2:
                        dve.wait_ge(edown_psum, n - 1)
                    nc.vector.tensor_tensor(htL[:, n % 2, :], p_turn, f32(htH[:, n % 2, :]), ALU.subtract).then_inc(eht_lo, 1)
                if stage == "down":
                    n, p, t = UNITS * b + m, m // J, m % J
                    dve.wait_ge(edown_psum, n + 1)
                    if p == 0:
                        nc.vector.tensor_copy(acc[:, t, :], p_part).then_inc(eacc_done, 1)
                    else:
                        dve.wait_ge(eacc_done, n - J + 1)
                        nc.vector.tensor_tensor(acc[:, t, :], acc[:, t, :], p_part, ALU.add).then_inc(eacc_done, 1)
                if (stage, m) == ("finish", 0):
                    dve.wait_ge(eacc_done, UNITS * (b + 1))
                    stats(lambda j: acc[:, j, :], EXPERTS_OWN)
                if (stage, m) == ("finish", 1):
                    link(rsqrt(ers[:, :], eva[:, :], ers[:, :], ert[:, :]))
                    for j in range(J):
                        step(nc.vector.tensor_scalar(acc[:, j, :], acc[:, j, :], emv[:, j, 0:1], ers[:, j:j + 1],
                                                     ALU.subtract, ALU.mult))
                    settle()
                    for j in range(J):
                        nc.vector.tensor_tensor(xb[:, j, :], xb[:, j, :], acc[:, j, :], ALU.add).then_inc(out_ready, 1)

            for name, b, m in steps("dve"):
                at(name, b, m)


def kernel(**inputs):
    import concourse.bacc as bacc
    from concourse.bass_utils import run_bass_kernel_spmd

    a = {k: np.ascontiguousarray(val) for k, val in inputs.items()}
    A, M = "L0_attn_", "L0_ffn_"

    def features(u):
        return np.reshape(u, (C, P, -1)).transpose(1, 0, 2)

    vecs = np.concatenate([features(a[A + n]) for n in ("ln1w", "ln1b")]
                          + [features(a[A + "conv_w"][:, 0, :])]
                          + [features(a[A + n]) for n in ("conv_b", "big", "bog")]
                          + [features(np.repeat(a[A + "bg"], HD))]
                          + [features(a[A + n]) for n in ("gnw", "gnb", "ln2w", "ln2b")], axis=2)
    headvecs = np.stack([a[A + n] for n in ("vnw", "vnb", "mnw", "mnb")])
    headvecs = np.broadcast_to(headvecs[None], (P, 4, HD))
    router = np.concatenate([a[M + "router_w"].T, a[M + "shared_gate_w"][:, None]], axis=1)
    def pairs(w, shared):
        slices = shared.reshape(D, SL, EI).transpose(1, 0, 2)
        both = np.concatenate([w, slices], axis=0)
        return both.reshape(PAIRS, 2, D, EI).transpose(0, 2, 1, 3).reshape(PAIRS, D, PW)

    up = np.concatenate([pairs(a[M + "w_gate"], a[M + "sw_gate"]), pairs(a[M + "w_up"], a[M + "sw_up"])], axis=2)
    up = up.reshape(PAIRS, C, P, 2 * PW).transpose(0, 2, 1, 3)
    down = np.concatenate([a[M + "w_down"].reshape(E * EI, D), a[M + "sw_down"]], axis=0).reshape(PAIRS, PW, D)

    arrays = {
        "x": a[A + "x"].reshape(T, D), "wq": a[A + "Wq"], "wk": a[A + "Wk"], "wv": a[A + "Wv"],
        "wig": a[A + "Wig"], "wog": a[A + "Wog"], "wo": a[A + "Wo"], "wg": a[A + "Wg"],
        "wgate": a[A + "Wgate"], "wval": a[A + "Wval"], "wout": a[A + "Wout"],
        "vecs": vecs, "headvecs": headvecs, "router": features(router), "up": up, "down": down,
    }
    arrays = {k: np.ascontiguousarray(val) for k, val in arrays.items()}
    nc = bacc.Bacc("TRN2", target_bir_lowering=False, num_devices=1)
    args = [nc.dram_tensor(k, val.shape, mybir.dt.from_np(val.dtype), kind="ExternalInput").ap()
            for k, val in arrays.items()]
    args.append(nc.dram_tensor("out", (T, D), F32, kind="ExternalOutput").ap())
    build(nc, *args)
    r = run_bass_kernel_spmd(nc, [arrays], core_ids=[0])
    return r.results[0]["out"].reshape(1, T, D)
```

```python
from contextlib import ExitStack

import numpy as np

import concourse.bass as bass
from concourse import mybir

P = 128
T, D = 2048, 256
C = D // P
TILES = (4, 4, 4, 4)
NB = len(TILES)
START = [sum(TILES[:b]) for b in range(NB + 1)]
BANKS = [(n + 1) // 2 for n in TILES]
BSTART = [sum(BANKS[:b]) for b in range(NB + 1)]
J = max(TILES)
TB = J * P
HEADS, HD = 16, 16
FF = 1024
FM = FF // P
KC = 4
E, EI, SI = 8, 176, 704
PAIRS = (E + SI // EI) // 2
PW = 2 * EI
PK = 3
LASTK = PW - 2 * P
CHUNK = [(2 * P, LASTK), (0, P), (P, P)]
ROUTED = E // 2
OUTPUTS = 2 * ROUTED + PAIRS - ROUTED
HIDDEN = FM + PK * PAIRS
DOWNS = FM + 2 * PAIRS
RW = E + 1
RP = RW + 1
EPS = 1e-5

F32, F32R, I32 = mybir.dt.float32, mybir.dt.float32r, mybir.dt.int32
ALU = mybir.AluOpType
ACT = mybir.ActivationFunctionType
AX_X = mybir.AxisListType.X

LN1W, LN1B, CONVW, CONVB, BIG, BOG, BG, GNW, GNB, LN2W, LN2B = 0, 1, 2, 6, 7, 8, 9, 10, 11, 12, 13
NVEC = 14


ATTENTION = (
    [("split", 2)] + [("q", j) for j in range(J)] + [("rs", 0), ("rs", 1), ("xs", 1), ("g", 0), ("g", 1)]
    + [("u", i) for i in range(4)] + [("split", 3), ("ut", 0), ("scan", 0), ("scan", 1), ("mt", 0), ("split", 4)]
    + [("var", 0), ("rstd", 0), ("norm", 0), ("fetch", 0), ("g", 2), ("affine", 0), ("affine", 1), ("split", 5)]
    + [("mean", 1), ("centre", 1), ("ln0", 0), ("var", 1), ("rstd", 1), ("split", 6), ("norm", 1), ("og", 0), ("y0", 0), ("ln0", 1)]
    + [("o", 0), ("o", 1), ("ln0", 2), ("wo", 0), ("ht", 0), ("ln2", 0), ("ln2", 1), ("h2", 0), ("ht", 1), ("conv", 0)]
    + [("h2", 1), ("conv", 1), ("conv", 2), ("conv", 3), ("xs", 0)])
AHEAD = [("ln0", i) for i in range(3)] + [("fetch", 0), ("ht", 0), ("ht", 1), ("xs", 0)] + [("conv", k) for k in range(KC)]


def _pair(p):
    ahead = [[("hid", PK * (p + 1) + i)] if p + 1 < PAIRS else [] for i in range(PK)]
    return (([("refill_dn", p + 1)] if p > 0 else []) + ahead[0] + [("dn", 2 * p), ("refill_up", p + 2)] + ahead[1]
            + [("dn", 2 * p + 1)] + ahead[2])


def _experts(nj):
    first = {3: ("refill_up", 0), 4: ("refill_dn", 0), 5: ("refill_up", 1), 6: ("refill_dn", 1)}
    start = [s for i in range(3) for s in (("hid", i), ("choose", i))]
    return ([("mup", 0)] + [s for m in range(1, FM) for s in [("mup", m), ("mdn", m - 1)] + ([first[m]] if m in first else [])]
            + [("mdn", FM - 1)] + [("sum", 0), ("sum", 1), ("x2", 0), ("x2", 1), ("xt", 0), ("hid", 0), ("route", 0)] + start[1:]
            + [("choose", 3)] + [s for p in range(PAIRS) for s in _pair(p)] + [("refill_dn", PAIRS + 1), ("finish", 0), ("finish", 1)])


EXPERTS = {nj: _experts(nj) for nj in set(TILES)}

PLACE = {
    "pe": [
        [0, 0, 0, 0, 0, 0, 0, 0, 0, 0, 0, 0, 0, 0, 0, 0, 0, 0, 0, 0, 0, 0, 0, 0, 0, 0, 0,
         0, 0, 0, 0, 0, 0, 0, 0, 0, 0, 0, 0, 0, 0, 0, 0, 0, 0, 0, 6, 6, 6, 7, 10, 10, 10],
        [16, 16, 18, 21, 22, 23, 23, 23, 24, 25, 26, 26, 26, 26, 27, 28, 33, 35, 36, 37, 39, 39, 39, 47, 50, 50, 57,
         57, 57, 57, 57, 57, 57, 57, 57, 57, 57, 63, 63, 64, 64, 64, 65, 66, 66, 67, 67, 72, 73, 74, 74, 74, 74],
        [75, 75, 75, 76, 82, 85, 90, 92, 94, 94, 94, 94, 94, 94, 94, 97, 98, 98, 99, 101, 105, 106, 109, 110, 110, 110, 110,
         110, 110, 110, 112, 112, 116, 119, 119, 119, 121, 121, 123, 124, 124, 124, 126, 128, 131, 133, 135, 135, 136, 137, 137, 137, 137],
        [138, 142, 145, 145, 150, 152, 164, 164, 168, 168, 168, 168, 170, 170, 171, 171, 171, 171, 173, 174, 179, 179, 189, 191, 192, 194, 194,
         194, 194, 194, 194, 202, 203, 207, 207, 208, 208, 208, 208, 209, 212, 214, 215, 220, 220, 222, 229, 242, 257, 268, 268, 275, 292],
    ],
    "act": [
        [0, 0, 0, 0, 0, 0, 0, 0, 0, 0, 0, 0, 0, 0, 0, 0, 0, 0, 0, 0, 0, 0, 0, 0, 0, 0, 0,
         0, 0, 0, 0, 0, 0, 0, 0, 0, 0, 0, 0, 0, 0, 0, 0, 0, 0, 0, 0, 0, 0, 10, 10, 11, 15],
        [16, 17, 19, 22, 22, 22, 22, 22, 24, 25, 26, 26, 26, 26, 27, 27, 31, 35, 35, 42, 44, 44, 44, 45, 48, 48, 48,
         48, 48, 50, 53, 54, 54, 54, 54, 55, 57, 58, 59, 59, 64, 64, 64, 65, 65, 67, 67, 67, 67, 69, 69, 69, 71],
        [71, 73, 74, 77, 80, 83, 90, 92, 92, 92, 92, 92, 92, 93, 93, 93, 96, 97, 99, 99, 104, 107, 108, 108, 108, 108, 108,
         108, 109, 111, 114, 115, 115, 115, 116, 118, 118, 118, 119, 119, 122, 126, 128, 131, 131, 133, 133, 134, 134, 137, 137, 137, 141],
        [142, 142, 144, 147, 151, 157, 157, 157, 166, 166, 169, 169, 177, 178, 184, 184, 184, 184, 184, 184, 184, 185, 187, 189, 191, 193, 195,
         195, 195, 195, 201, 202, 202, 206, 209, 209, 209, 209, 209, 210, 211, 214, 217, 217, 217, 217, 217, 217, 217, 218, 218, 218, 239],
    ],
    "dve": [
        [0, 0, 0, 0, 0, 0, 0, 0, 0, 0, 0, 0, 0, 0, 0, 0, 0, 0, 0, 0, 0, 0, 0, 0, 0, 0, 0,
         0, 0, 0, 0, 0, 0, 0, 0, 0, 0, 0, 0, 0, 0, 0, 0, 0, 0, 0, 0, 0, 0, 2, 7, 8, 14],
        [19, 20, 20, 24, 24, 24, 24, 24, 25, 25, 25, 25, 25, 25, 25, 26, 28, 29, 31, 35, 36, 36, 36, 37, 39, 39, 40,
         44, 46, 47, 50, 50, 51, 52, 54, 54, 57, 57, 57, 59, 61, 63, 63, 63, 64, 65, 66, 66, 67, 68, 68, 68, 68],
        [77, 77, 77, 78, 80, 83, 88, 88, 90, 90, 90, 93, 93, 94, 94, 94, 98, 98, 99, 99, 99, 102, 103, 103, 104, 106, 110,
         110, 110, 110, 110, 112, 114, 115, 116, 116, 117, 117, 119, 119, 121, 122, 123, 124, 124, 133, 134, 134, 134, 137, 137, 137, 137],
        [142, 143, 149, 150, 151, 153, 154, 155, 161, 163, 165, 168, 168, 168, 170, 170, 172, 172, 175, 182, 188, 188, 188, 188, 188, 190, 191,
         191, 191, 191, 198, 202, 202, 205, 206, 206, 206, 207, 209, 209, 209, 210, 211, 217, 217, 219, 219, 219, 221, 222, 222, 223, 229],
    ],
    "pool": [
        [0, 0, 0, 0, 0, 0, 0, 0, 0, 0, 0, 0, 0, 0, 0, 0, 0, 0, 0, 0, 0, 0, 0, 0, 0, 0, 0,
         0, 0, 0, 0, 0, 0, 0, 0, 0, 1, 1, 1, 1, 1, 1, 1, 1, 1, 1, 5, 10, 10, 11, 23, 23, 23],
        [23, 23, 24, 24, 24, 24, 24, 24, 24, 25, 25, 25, 25, 25, 25, 25, 25, 31, 31, 31, 32, 32, 32, 42, 53, 54, 54,
         54, 54, 54, 54, 54, 55, 55, 55, 55, 55, 55, 55, 55, 60, 60, 62, 62, 68, 68, 69, 71, 71, 72, 72, 72, 72],
        [86, 86, 86, 86, 86, 89, 92, 92, 92, 93, 94, 94, 94, 94, 97, 97, 99, 99, 99, 99, 100, 100, 100, 100, 100, 100, 100,
         100, 100, 100, 100, 100, 100, 100, 102, 102, 111, 111, 112, 113, 114, 124, 124, 126, 126, 129, 132, 142, 142, 145, 150, 150, 150],
        [156, 156, 159, 159, 160, 160, 162, 162, 162, 162, 162, 162, 162, 162, 168, 173, 173, 176, 176, 193, 194, 194, 221, 221, 221, 221, 221,
         223, 223, 223, 223, 234, 234, 234, 234, 234, 234, 234, 246, 248, 249, 259, 267, 268, 270, 270, 272, 281, 282, 283, 286, 286, 291],
    ],
}


def steps(engine):
    attention = [(PLACE[engine][b][i] if b >= 0 else 0, s[0], b + (s in AHEAD), s[1]) for b in range(-1, NB)
                 for i, s in enumerate(ATTENTION) if 0 <= b + (s in AHEAD) < NB]
    experts = [(name, b, m) for b in range(NB) for name, m in EXPERTS[TILES[b]]]
    for n, step in enumerate(experts):
        while attention and attention[0][0] <= n:
            yield attention.pop(0)[1:]
        yield step


def build(nc, x, wq, wk, wv, wig, wog, wo, wg, wgate, wval, wout, vecs, headvecs, router, up, down, out):
    ctx = ExitStack()
    with ctx:
        def sem(name):
            return ctx.enter_context(nc.semaphore(name))

        def sb(name, shape, dt=F32):
            return ctx.enter_context(nc.sbuf_tensor(name, shape, dt))

        psum = ctx.enter_context(nc.psum_tensor("psum", [P, 8, 512], F32))
        p_main, p_down = psum[:, 0:2, :], psum[:, 6:8, :]
        p_route = psum[:, 6, 0:J * RP]

        def p_pair(n):
            return psum[:, 2 + 2 * (n % 2), :], psum[:, 3 + 2 * (n % 2), :]

        shapes = {"qkv": [P, C, 3 * D], "gw": [P, C, 2 * D], "wo": [P, C, D], "wgt": [P, C, FF],
                  "wvl": [P, C, FF], "wou": [P, FM, D], "up": [P, 2, C, 2 * PW], "dn": [P, 2, 2 * 2, D],
                  "hm": [P, 3, TB]}
        with ExitStack() as first_names:
            raw = {k: first_names.enter_context(nc.sbuf_tensor(k + "R", s, F32)) for k, s in shapes.items()}
        lo = {k: sb(k + "L", s, F32R) for k, s in shapes.items()}
        hi = {k: sb(k + "H", s, F32R) for k, s in shapes.items()}

        ident = sb("ident", [P, P])
        centring = sb("centring", [P, P])
        hst, hmv = sb("hst", [P, J, 6]), sb("hmv", [P, J, 2])
        hva, hrs, hrt = (sb(k, [P, J]) for k in ("hva", "hrs", "hrt"))
        vec = sb("vec", [P, C, NVEC])
        hvec = sb("hvec", [P, 4, HD])
        wr, wrH, wrL = sb("wr", [P, C, RP]), sb("wrH", [P, C, RP], F32R), sb("wrL", [P, C, RP], F32R)
        wg16, wgx = sb("wg16", [P, C, HEADS]), sb("wgx", [P, C, D])
        wmean = sb("wmean", [P, C, HEADS])
        st, mv = sb("st", [P, J, 6]), sb("mv", [P, J, 2])
        est, emv = sb("est", [P, J, 6]), sb("emv", [P, J, 2])
        eva, ers, ert = (sb(k, [P, J]) for k in ("eva", "ers", "ert"))
        va, rs, rt = (sb(k, [P, J * 3 * HEADS]) for k in ("va", "rs", "rt"))
        r0, n0 = sb("r0", [P, 2, J]), sb("n0", [P, 2, J])
        s1, n1 = sb("s1", [P, J]), sb("n1", [P, J])
        l2r, l2n, x2r, x2n = (sb(k, [P, J]) for k in ("l2r", "l2n", "x2r", "x2n"))
        rr, mu, carry = sb("rr", [P, J, 3 * HEADS]), sb("mu", [P, J * HEADS]), sb("carry", [P, C])
        LG, ex, key = sb("LG", [P, J, RW]), sb("ex", [P, J, RW]), sb("key", [P, J, E])
        pick, top, rank = sb("pick", [P, 2, J, E]), sb("top", [P, 4, J]), sb("rank", [P, E])
        cw = sb("cw", [P, J, RW])
        X = sb("X", [P, 2, J, D])
        HN = sb("HN", [P, J, D])
        HT = sb("HT", [P, C, KC - 1 + TB])
        AH, AL = sb("AH", [P, C, TB], F32R), sb("AL", [P, C, TB], F32R)
        QKV = sb("QKV", [P, J, 3 * D])
        XC = sb("XC", [P, C, TB])
        IG, OG, GA = sb("IG", [P, C, TB]), sb("OG", [P, C, TB]), sb("GA", [P, C, TB])
        HR = sb("HR", [P, J, D])
        H2H, H2L = sb("H2H", [P, C, TB], F32R), sb("H2L", [P, C, TB], F32R)
        SQ = [G[:, :, :].rearrange("p c t -> p (c t)")[:, 0:3 * D] for G in (IG, OG)]
        MSQ = IG[:, :, :].rearrange("p c t -> p (c t)")
        XTH, XTL = sb("XTH", [P, C, TB], F32R), sb("XTL", [P, C, TB], F32R)
        acc = sb("acc", [P, J, D])

        SM, HMH, HML = raw["hm"], hi["hm"], lo["hm"]

        x_in = [sem(f"x_in{i}") for i in range(2)]
        h_in, carry_kept, wr_hi, wr_lo = map(sem, ("h_in", "carry_kept", "wr_hi", "wr_lo"))
        const_in, stored = sem("const_in"), sem("stored")
        w_in = {k: sem(k + "_in") for k in ("qkv", "v", "gw", "wo", "wgt", "wvl", "wou")}
        up_in, dn_in = ([sem(f"{k}_in{i}") for i in range(2)] for k in ("up", "dn"))
        w_centred, w_hi, w_lo, wg_ready = map(sem, ("w_centred", "w_hi", "w_lo", "wg_ready"))
        up_hi, up_lo, dn_hi, dn_lo = map(sem, ("up_hi", "up_lo", "dn_hi", "dn_lo"))
        ident_zero, ident_ready, halo_zero, same_head = map(sem, ("ident_zero", "ident_ready", "halo_zero", "same_head"))
        s_dve, s_act, s_pool = sem("s_dve"), sem("s_act"), sem("s_pool")
        ln0_ready, hn_ready, ht_psum, ht_ready, ht_hi, ht_lo = map(
            sem, ("ln0_ready", "hn_ready", "ht_psum", "ht_ready", "ht_hi", "ht_lo"))
        conv_done, conv_hi, conv_lo = map(sem, ("conv_done", "conv_hi", "conv_lo"))
        qkv_psum, qkv_copied, sq_ready, ss_done, v_scaled = map(
            sem, ("qkv_psum", "qkv_copied", "sq_ready", "ss_done", "v_scaled"))
        gate_psum, gate_ready = sem("gate_psum"), sem("gate_ready")
        rr_ready, u_ready, g_ready, ut_psum, mem_ready, mem_psum = map(
            sem, ("rr_ready", "u_ready", "g_ready", "ut_psum", "mem_ready", "mem_psum"))
        centring_ready, normed, centred, msq_ready, og_ready, og_psum, og_affine, o_ready, o_hi, o_lo = map(
            sem, ("centring_ready", "normed", "centred", "msq_ready", "og_ready", "og_psum", "og_affine", "o_ready", "o_hi", "o_lo"))
        y0_ready, wo_psum, hr_ready, ln2_stats, hn2_ready, h2_psum, h2_hi, h2_lo = map(
            sem, ("y0_ready", "wo_psum", "hr_ready", "ln2_stats", "hn2_ready", "h2_psum", "h2_hi", "h2_lo"))
        up_psum, silu_ready, hid_ready, hid_hi, hid_lo, down_psum = map(
            sem, ("up_psum", "silu_ready", "hid_ready", "hid_hi", "hid_lo", "down_psum"))
        x2_stats, xn_ready, xt_psum, xt_hi, xt_lo, rt_psum, rt_copied = map(
            sem, ("x2_stats", "xn_ready", "xt_psum", "xt_hi", "xt_lo", "rt_psum", "rt_copied"))
        lmax_ready, exp_ready, eacc_done = map(sem, ("lmax_ready", "exp_ready", "eacc_done"))
        out_ready = sem("out_ready")

        def f32(ap):
            return ap.bitcast(F32)

        def heads(ap):
            return ap.rearrange("p j (h d) -> p j h d", d=HD)

        def per_head(ap):
            return ap.unsqueeze(3).broadcast_to([P, ap.shape[1], HEADS, HD])

        def per_dim(nj, i):
            return hvec[:, i, :].unsqueeze(1).unsqueeze(1).broadcast_to([P, nj, HEADS, HD])

        def v(c, i):
            return vec[:, c, i:i + 1]

        def downs(b, step):
            return DOWNS * BSTART[b] + (step + 1) * BANKS[b]

        def place(m):
            if m < FM:
                return m % 3, m
            p, i = divmod(m - FM, PK)
            return (p + i) % 3, FM + 2 * p + (i != 1)

        freed, user = [], [0, 0, 0]
        for g in range(NB * HIDDEN):
            at_place, down_step = place(g % HIDDEN)
            freed.append(user[at_place])
            user[at_place] = downs(g // HIDDEN, down_step)

        resident = [("qkv", slice(0, 2 * D), "qkv", 32), ("qkv", slice(2 * D, 3 * D), "v", 16), ("gw", slice(0, 2 * D), "gw", 32),
                    ("wo", slice(0, D), "wo", 16), ("wgt", slice(0, FF), "wgt", 16), ("wvl", slice(0, FF), "wvl", 16),
                    ("wou", slice(0, D), "wou", 16)]
        W_QKV, W_GATES, W_O, W_UP, W_OUT = 2, 3, 4, 6, 7

        def hidden(stage, b, m):
            m, rows = (m, P) if stage == "mup" else (FM + m, CHUNK[m % PK][1])
            return HIDDEN * b + m, place(m)[0], rows

        block = ctx.enter_context(nc.Block())

        @block.sync
        def _(sp):
            def rows(w):
                return w.rearrange("(c p) n -> p c n", p=P)

            def load_x(b):
                sp.dma_start(X[:, b % 2, 0:TILES[b], :],
                             x[START[b] * P:START[b + 1] * P, :].rearrange("(j p) d -> p j d", p=P)).then_inc(x_in[b % 2], 16)

            def load_up(g):
                if g >= 2:
                    sp.wait_ge(up_psum, (g - 2) // PAIRS * HIDDEN + FM + PK * ((g - 2) % PAIRS + 1))
                sp.dma_start(raw["up"][:, g % 2], up[g % PAIRS]).then_inc(up_in[g % 2], 16)

            def load_dn(g):
                if g >= 2:
                    sp.wait_ge(down_psum, downs((g - 2) // PAIRS, FM + 2 * ((g - 2) % PAIRS) + 1))
                sp.dma_start(raw["dn"][:, g % 2], down[g % PAIRS]).then_inc(dn_in[g % 2], 16)

            def store(b):
                sp.wait_ge(out_ready, START[b + 1])
                sp.dma_start(out[START[b] * P:START[b + 1] * P, :].rearrange("(j p) d -> p j d", p=P),
                             X[:, b % 2, 0:TILES[b], :]).then_inc(stored, 16)
                sp.wait_ge(stored, 16 * (b + 1))

            sp.dma_start(QKV[:, 0:TILES[0], 0:D], x[0:START[1] * P, :].rearrange("(j p) d -> p j d", p=P)).then_inc(h_in, 16)
            sp.dma_start(raw["qkv"][:, :, 2 * D:3 * D], rows(wv)).then_inc(w_in["v"], 16)
            sp.dma_start(raw["qkv"][:, :, 0:D], rows(wq)).then_inc(w_in["qkv"], 16)
            sp.dma_start(raw["qkv"][:, :, D:2 * D], rows(wk)).then_inc(w_in["qkv"], 16)
            sp.dma_start(vec[:, :, :], vecs).then_inc(const_in, 16)
            sp.dma_start(hvec[:, :, :], headvecs).then_inc(const_in, 16)
            sp.dma_start(wg16[:, :, :], rows(wg)).then_inc(const_in, 16)
            sp.dma_start(wr[:, :, :], router).then_inc(const_in, 16)
            sp.dma_start(raw["gw"][:, :, 0:D], rows(wig)).then_inc(w_in["gw"], 16)
            sp.dma_start(raw["gw"][:, :, D:2 * D], rows(wog)).then_inc(w_in["gw"], 16)
            sp.dma_start(raw["wo"][:, :, :], rows(wo)).then_inc(w_in["wo"], 16)
            sp.dma_start(raw["wgt"][:, :, :], rows(wgate)).then_inc(w_in["wgt"], 16)
            sp.dma_start(raw["wvl"][:, :, :], rows(wval)).then_inc(w_in["wvl"], 16)
            sp.dma_start(raw["wou"][:, :, :], rows(wout)).then_inc(w_in["wou"], 16)
            load_x(0)
            load_x(1)
            G = NB * PAIRS
            for g in range(G):
                load_up(g)
                load_dn(g)
                if g % PAIRS == 1 and g > PAIRS:
                    store(g // PAIRS - 1)
                    if g // PAIRS + 1 < NB:
                        load_x(g // PAIRS + 1)
            store(NB - 1)

        @block.gpsimd
        def _(pool):
            n_pool = [0]

            def link(ins):
                n_pool[0] += 1
                ins.then_inc(s_pool, 1)
                pool.wait_ge(s_pool, n_pool[0])

            nc.gpsimd.memset(ident[:, :], 0.0).then_inc(ident_zero, 1)
            pool.wait_ge(ident_zero, 1)
            nc.gpsimd.affine_select(out=ident[:, :], in_=ident[:, :], compare_op=ALU.not_equal, fill=1.0, base=0,
                                    pattern=[[-1, P]], channel_multiplier=1).then_inc(ident_ready, 1)
            link(nc.gpsimd.memset(centring[:, :], 1.0))
            by_heads = centring[:, :].rearrange("p (h d) -> p h d", d=HD)
            link(nc.gpsimd.affine_select(out=by_heads, in_=by_heads, compare_op=ALU.is_ge, fill=0.0, base=0,
                                         pattern=[[-HD, P // HD], [0, HD]], channel_multiplier=1))
            nc.gpsimd.affine_select(out=by_heads, in_=by_heads, compare_op=ALU.is_ge, fill=0.0, base=HD - 1,
                                    pattern=[[HD, P // HD], [0, HD]], channel_multiplier=-1).then_inc(same_head, 1)

            def split(i):
                k, cols, _, _ = resident[i]
                pool.wait_ge(w_hi, i + 1)
                nc.gpsimd.tensor_tensor(lo[k][:, :, cols], raw[k][:, :, cols], f32(hi[k][:, :, cols]),
                                        ALU.subtract).then_inc(w_lo, 1)

            def split_up(g):
                pool.wait_ge(up_hi, g + 1)
                nc.gpsimd.tensor_tensor(lo["up"][:, g % 2], raw["up"][:, g % 2], f32(hi["up"][:, g % 2]),
                                        ALU.subtract).then_inc(up_lo, 1)

            def split_dn(g):
                pool.wait_ge(dn_hi, g + 1)
                nc.gpsimd.tensor_tensor(lo["dn"][:, g % 2], raw["dn"][:, g % 2], f32(hi["dn"][:, g % 2]),
                                        ALU.subtract).then_inc(dn_lo, 1)

            split(0)
            split(1)

            def at(stage, b, m):
                nj, old, new = TILES[b], START[b], START[b + 1]
                tb = nj * P
                if (stage, m) == ("ht", 1):
                    for c in range(C):
                        pool.wait_ge(ht_hi, C * b + c + 1)
                        nc.gpsimd.tensor_tensor(AL[:, c, 0:tb], HT[:, c, KC - 1:KC - 1 + tb], f32(AH[:, c, 0:tb]),
                                                ALU.subtract).then_inc(ht_lo, 1)
                if stage == "q" and m < nj:
                    pool.wait_ge(sq_ready, old + m + 1)
                    vj = QKV[:, m, 2 * D:3 * D].rearrange("p (h d) -> p h d", d=HD)
                    nc.gpsimd.tensor_tensor(vj, vj, hvec[:, 0, :].unsqueeze(1).broadcast_to([P, HEADS, HD]),
                                            ALU.mult).then_inc(v_scaled, 1)
                if (stage, m) == ("xs", 1):
                    for c in range(C):
                        pool.wait_ge(conv_hi, C * b + c + 1)
                        nc.gpsimd.tensor_tensor(AL[:, c, 0:tb], XC[:, c, 0:tb], f32(AH[:, c, 0:tb]),
                                                ALU.subtract).then_inc(conv_lo, 1)
                if stage == "scan":
                    q, k, w = (heads(QKV[:, 0:nj, i * D:(i + 1) * D]) for i in range(3))
                    if m == 0:
                        pool.wait_ge(rr_ready, b + 1)
                        link(nc.gpsimd.tensor_tensor(q, q, per_head(rr[:, 0:nj, 0:HEADS]), ALU.mult))
                        pool.wait_ge(u_ready, b + 1)
                        nc.gpsimd.tensor_tensor(k, q, per_dim(nj, 2), ALU.mult).then_inc(g_ready, 1)
                    else:
                        pool.wait_ge(ut_psum, b + 1)
                        nc.gpsimd.tensor_tensor(w, q, per_dim(nj, 3), ALU.mult).then_inc(g_ready, 1)
                if stage in ("mup", "hid"):
                    g, i, rows = hidden(stage, b, m)
                    pool.wait_ge(hid_hi, g + 1)
                    nc.gpsimd.tensor_tensor(HML[0:rows, i, 0:tb], SM[0:rows, i, 0:tb], f32(HMH[0:rows, i, 0:tb]),
                                            ALU.subtract).then_inc(hid_lo, 1)
                if stage == "split" and b == 0:
                    if m == 2:
                        pool.wait_ge(wr_hi, 1)
                        nc.gpsimd.tensor_tensor(wrL[:, :, :], wr[:, :, :], f32(wrH[:, :, :]), ALU.subtract).then_inc(wr_lo, 1)
                    split(m)
                if stage == "refill_up" and (b == 0 or m >= 2) and b * PAIRS + m < NB * PAIRS:
                    split_up(b * PAIRS + m)
                if stage == "refill_dn" and (b == 0 or m >= 2) and b * PAIRS + m < NB * PAIRS:
                    split_dn(b * PAIRS + m)

            for name, b, m in steps("pool"):
                at(name, b, m)

        @block.scalar
        def _(act):
            n_act = [0]

            def step(ins):
                n_act[0] += 1
                ins.then_inc(s_act, 1)

            def settle():
                act.wait_ge(s_act, n_act[0])

            def split(i):
                k, cols, arrival, count = resident[i]
                act.wait_ge(w_in[arrival], count)
                if arrival == "v":
                    act.wait_ge(w_centred, 1)
                nc.scalar.activation(hi[k][:, :, cols], raw[k][:, :, cols], ACT.Copy).then_inc(w_hi, 1)

            def split_up(g):
                act.wait_ge(up_in[g % 2], 16 * (g // 2 + 1))
                nc.scalar.activation(hi["up"][:, g % 2], raw["up"][:, g % 2], ACT.Copy).then_inc(up_hi, 1)

            def split_dn(g):
                act.wait_ge(dn_in[g % 2], 16 * (g // 2 + 1))
                nc.scalar.activation(hi["dn"][:, g % 2], raw["dn"][:, g % 2], ACT.Copy).then_inc(dn_hi, 1)

            split(0)

            def at(stage, b, m):
                nj, old, new = TILES[b], START[b], START[b + 1]
                tb = nj * P
                if stage == "fetch" and b > 0:
                    act.wait_ge(g_ready, 2 * b)
                    act.dma_start(QKV[:, 0:nj, 0:D], x[old * P:new * P, :].rearrange("(j p) d -> p j d", p=P)).then_inc(h_in, 16)
                if (stage, m) == ("ln0", 2):
                    act.wait_ge(ln0_ready, b + 1)
                    for j in range(nj):
                        nc.scalar.activation(QKV[:, j, 0:D], QKV[:, j, 0:D], ACT.Identity, bias=n1[:, j:j + 1],
                                             scale=s1[:, j:j + 1]).then_inc(hn_ready, 1)
                    if b == 0:
                        split(1)
                if (stage, m) == ("ht", 0):
                    if b == 0:
                        act.wait_ge(const_in, 64)
                        nc.scalar.activation(wrH[:, :, :], wr[:, :, :], ACT.Copy).then_inc(wr_hi, 1)
                        act.wait_ge(halo_zero, 1)
                    else:
                        act.wait_ge(conv_done, C * b)
                        act.wait_ge(ht_lo, C * b)
                        end = TILES[b - 1] * P
                        step(nc.scalar.activation(HT[:, :, 0:KC - 1], HT[:, :, end:end + KC - 1], ACT.Copy))
                        settle()
                    act.wait_ge(ht_psum, b + 1)
                    for c in range(C):
                        nc.scalar.activation(HT[:, c, KC - 1:KC - 1 + tb], p_main[:, c, 0:tb], ACT.Identity, bias=v(c, LN1B),
                                             scale=v(c, LN1W)).then_inc(ht_ready, 1)
                if (stage, m) == ("ht", 1):
                    if b > 0:
                        act.wait_ge(wo_psum, b)
                    for c in range(C):
                        act.wait_ge(ht_ready, C * b + c + 1)
                        nc.scalar.activation(AH[:, c, 0:tb], HT[:, c, KC - 1:KC - 1 + tb], ACT.Copy).then_inc(ht_hi, 1)
                if stage == "q" and m < nj:
                    n = old + m
                    act.wait_ge(qkv_psum, n + 1)
                    nc.scalar.activation(QKV[:, m, :], p_main.rearrange("p a n -> p (a n)")[:, 0:3 * D],
                                         ACT.Copy).then_inc(qkv_copied, 1)
                    act.wait_ge(qkv_copied, n + 1)
                    if n >= 2:
                        act.wait_ge(ss_done, n - 1)
                    nc.scalar.activation(SQ[n % 2], QKV[:, m, :], ACT.Square).then_inc(sq_ready, 1)
                if (stage, m) == ("xs", 0):
                    for c in range(C):
                        act.wait_ge(conv_done, C * b + c + 1)
                        step(nc.scalar.activation(XC[:, c, 0:tb], XC[:, c, 0:tb], ACT.Silu))
                if (stage, m) == ("xs", 1):
                    settle()
                    act.wait_ge(qkv_psum, new)
                    for c in range(C):
                        nc.scalar.activation(AH[:, c, 0:tb], XC[:, c, 0:tb], ACT.Copy).then_inc(conv_hi, 1)
                if stage == "g":
                    dst, bias = ((IG, BIG), (GA, BG), (OG, BOG))[m]
                    if m == 0:
                        act.wait_ge(ss_done, new)
                        if b > 0:
                            act.wait_ge(h2_lo, C * b)
                    for c in range(C):
                        act.wait_ge(gate_psum, C * (3 * b + m) + c + 1)
                        nc.scalar.activation(dst[:, c, 0:tb], p_main[:, c, 0:tb], ACT.Sigmoid,
                                             bias=v(c, bias)).then_inc(gate_ready, 1)
                if stage == "mt":
                    act.wait_ge(mem_psum, b + 1)
                    act.wait_ge(carry_kept, b + 1)
                    nc.scalar.activation(MSQ[:, 0:nj * D], p_main.rearrange("p a n -> p (a n)")[:, 0:nj * D],
                                         ACT.Square).then_inc(msq_ready, 1)
                if stage == "centre":
                    act.wait_ge(centred, b + 1)
                    nc.scalar.activation(MSQ[:, 0:nj * D], HN[:, 0:nj, :].rearrange("p j d -> p (j d)"),
                                         ACT.Square).then_inc(msq_ready, 1)
                if (stage, m) == ("og", 0):
                    act.wait_ge(og_psum, b + 1)
                    for c in range(C):
                        nc.scalar.activation(GA[:, c, 0:tb], p_main[:, c, 0:tb], ACT.Identity, bias=v(c, GNB),
                                             scale=v(c, GNW)).then_inc(og_affine, 1)
                if (stage, m) == ("o", 0):
                    for c in range(C):
                        act.wait_ge(o_ready, C * b + c + 1)
                        nc.scalar.activation(AH[:, c, 0:tb], OG[:, c, 0:tb], ACT.Copy).then_inc(o_hi, 1)
                if stage == "y0":
                    act.wait_ge(og_psum, b + 1)
                    act.wait_ge(x_in[b % 2], 16 * (b // 2 + 1))
                    for j in range(nj):
                        nc.scalar.activation(HN[:, j, :], X[:, b % 2, j, :], ACT.Identity, bias=n0[:, b % 2, j:j + 1],
                                             scale=r0[:, b % 2, j:j + 1]).then_inc(y0_ready, 1)
                if (stage, m) == ("ln2", 1):
                    act.wait_ge(ln2_stats, b + 1)
                    for j in range(nj):
                        nc.scalar.activation(HN[:, j, :], HR[:, j, :], ACT.Identity, bias=l2n[:, j:j + 1],
                                             scale=l2r[:, j:j + 1]).then_inc(hn2_ready, 1)
                if (stage, m) == ("h2", 0):
                    act.wait_ge(h2_psum, b + 1)
                    for c in range(C):
                        step(nc.scalar.activation(GA[:, c, 0:tb], p_main[:, c, 0:tb], ACT.Identity, bias=v(c, LN2B),
                                                  scale=v(c, LN2W)))
                if (stage, m) == ("h2", 1):
                    settle()
                    if b > 0:
                        act.wait_ge(up_psum, HIDDEN * (b - 1) + FM)
                    for c in range(C):
                        nc.scalar.activation(H2H[:, c, 0:tb], GA[:, c, 0:tb], ACT.Copy).then_inc(h2_hi, 1)
                if stage in ("mup", "hid"):
                    g, i, rows = hidden(stage, b, m)
                    act.wait_ge(up_psum, g + 1)
                    if freed[g]:
                        act.wait_ge(down_psum, freed[g])
                    nc.scalar.activation(SM[0:rows, i, 0:tb], p_pair(g)[0][0:rows, 0:tb], ACT.Silu).then_inc(silu_ready, 1)
                    act.wait_ge(hid_ready, g + 1)
                    nc.scalar.activation(HMH[0:rows, i, 0:tb], SM[0:rows, i, 0:tb], ACT.Copy).then_inc(hid_hi, 1)
                if (stage, m) == ("x2", 1):
                    act.wait_ge(x2_stats, b + 1)
                    for j in range(nj):
                        nc.scalar.activation(HR[:, j, :], X[:, b % 2, j, :], ACT.Identity, bias=x2n[:, j:j + 1],
                                             scale=x2r[:, j:j + 1]).then_inc(xn_ready, 1)
                if stage == "xt":
                    act.wait_ge(xt_psum, b + 1)
                    for c in range(C):
                        nc.scalar.activation(XTH[:, c, 0:tb], p_down[:, c, 0:tb], ACT.Copy).then_inc(xt_hi, 1)
                if (stage, m) == ("choose", 0):
                    act.wait_ge(lmax_ready, b + 1)
                    nc.scalar.activation(ex[:, 0:nj, :], ex[:, 0:nj, :], ACT.Exp).then_inc(exp_ready, 1)
                if stage == "split" and b == 0:
                    split(m)
                if stage == "refill_up" and (b == 0 or m >= 2) and b * PAIRS + m < NB * PAIRS:
                    split_up(b * PAIRS + m)
                if stage == "refill_dn" and (b == 0 or m >= 2) and b * PAIRS + m < NB * PAIRS:
                    split_dn(b * PAIRS + m)

            for name, b, m in steps("act"):
                at(name, b, m)

        @block.tensor
        def _(pe):
            def mm3(dst, aH, aL, bH, bL, start, stop, shared=False):
                nc.tensor.matmul(dst, aH, bH, start=start, stop=False, skip_group_check=shared)
                nc.tensor.matmul(dst, aH, bL, start=False, stop=False, skip_group_check=shared)
                return nc.tensor.matmul(dst, aL, bH, start=False, stop=stop, skip_group_check=shared)

            def to_features(dst, src, nj, ready=None, before=0):
                for j in range(nj):
                    if ready is not None:
                        pe.wait_ge(ready, before + j + 1)
                    for c in range(C):
                        last = nc.tensor.transpose(dst[:, c, j * P:(j + 1) * P], src(j)[:, c * P:(c + 1) * P], ident[:, :])
                return last

            pe.wait_ge(ident_ready, 1)

            def up_product(b, m, features, rows, weight):
                g, tb = HIDDEN * b + m, TILES[b] * P
                if g >= 2:
                    pe.wait_ge(hid_ready, g - 1)
                for half, dst in enumerate(p_pair(g)):
                    for c in range(C):
                        last = mm3(dst[0:rows, 0:tb], weight(half, hi, c), weight(half, lo, c), features[0][:, c, 0:tb],
                                   features[1][:, c, 0:tb], c == 0, c == C - 1)
                last.then_inc(up_psum, 1)

            def mlp_down(b, m):
                i, nj = place(m)[0], TILES[b]
                pe.wait_ge(hid_lo, HIDDEN * b + m + 1)
                for j in range(nj):
                    cols = slice(j * P, (j + 1) * P)
                    last = mm3(p_down[:, j // 2, (j % 2) * D:(j % 2 + 1) * D], HMH[:, i, cols], HML[:, i, cols],
                               hi["wou"][:, m, :], lo["wou"][:, m, :], m == 0 and j % 2 == 0, m == FM - 1, shared=True)
                    if j % 2 == 1 or j == nj - 1:
                        last.then_inc(down_psum, 1)

            def expert_down(b, d):
                nj, p, half = TILES[b], d // 2, d % 2
                ring = p % 2
                parts = [(1 + half, half), (0, 2 + half)] if p < ROUTED else [[(1, 0)], [(2, 1), (0, 2)]][half]
                o = 2 * p + half if p < ROUTED else ROUTED + p
                opens, closes = p < ROUTED or half == 0, p < ROUTED or half == 1
                if half == 0:
                    pe.wait_ge(dn_lo, b * PAIRS + p + 1)
                if d == 0:
                    pe.wait_ge(rt_copied, b + 1)
                pe.wait_ge(hid_lo, HIDDEN * b + FM + PK * p + 2 + half)
                for j in range(nj):
                    if opens and j % 2 == 0 and o > 0:
                        pe.wait_ge(eacc_done, OUTPUTS * START[b] + (o - 1) * nj + min(j + 2, nj))
                    cols = slice(j * P, (j + 1) * P)
                    for k, (chunk, w) in enumerate(parts):
                        rows, i = CHUNK[chunk][1], place(FM + PK * p + chunk)[0]
                        last = mm3(p_down[:, j // 2, (j % 2) * D:(j % 2 + 1) * D], HMH[0:rows, i, cols], HML[0:rows, i, cols],
                                   hi["dn"][0:rows, ring, w, :], lo["dn"][0:rows, ring, w, :],
                                   opens and k == 0 and j % 2 == 0, closes and k == len(parts) - 1, shared=True)
                    if j % 2 == 1 or j == nj - 1:
                        last.then_inc(down_psum, 1)

            def at(stage, b, m):
                nj, old, new = TILES[b], START[b], START[b + 1]
                tb = nj * P
                if (stage, m) == ("ht", 0):
                    if b > 0:
                        pe.wait_ge(hr_ready, b)
                    to_features(p_main, lambda j: QKV[:, j, 0:D], nj, hn_ready, old).then_inc(ht_psum, 1)
                if stage == "q" and m < nj:
                    n = old + m
                    if m == 0:
                        if b == 0:
                            pe.wait_ge(w_lo, W_QKV)
                        pe.wait_ge(ht_lo, C * (b + 1))
                    else:
                        pe.wait_ge(qkv_copied, n)
                    tok = slice(m * P, (m + 1) * P)
                    for part, cols in ((0, slice(0, 2 * D)), (1, slice(2 * D, 3 * D))):
                        for c in range(C):
                            last = mm3(p_main[:, part, 0:cols.stop - cols.start], AH[:, c, tok], AL[:, c, tok],
                                       hi["qkv"][:, c, cols], lo["qkv"][:, c, cols], c == 0, c == C - 1)
                    last.then_inc(qkv_psum, 1)
                if stage == "g":
                    if m == 0:
                        pe.wait_ge(qkv_copied, new)
                        if b == 0:
                            pe.wait_ge(w_lo, W_GATES)
                            pe.wait_ge(wg_ready, 1)
                        pe.wait_ge(conv_lo, C * (b + 1))
                    if m == 2:
                        pe.wait_ge(normed, b + 1)
                    for o in range(C):
                        if m == 1:
                            pe.wait_ge(gate_ready, C * 3 * b + o + 1)
                        for c in range(C):
                            if m == 1:
                                last = nc.tensor.matmul(p_main[:, o, 0:tb], wgx[:, c, o * P:(o + 1) * P], XC[:, c, 0:tb],
                                                        start=c == 0, stop=c == C - 1)
                            else:
                                cols = slice(m // 2 * D + o * P, m // 2 * D + (o + 1) * P)
                                last = mm3(p_main[:, o, 0:tb], hi["gw"][:, c, cols], lo["gw"][:, c, cols],
                                           AH[:, c, 0:tb], AL[:, c, 0:tb], c == 0, c == C - 1)
                        last.then_inc(gate_psum, 1)
                if stage == "ut":
                    pe.wait_ge(u_ready, b + 1)
                    pe.wait_ge(gate_ready, C * (3 * b + 2))
                    to_features(p_main, lambda j: QKV[:, j, 2 * D:3 * D], nj).then_inc(ut_psum, 1)
                if stage == "mt":
                    pe.wait_ge(mem_ready, C * (b + 1))
                    if b == 0:
                        pe.wait_ge(centring_ready, 1)
                    for j in range(nj):
                        for c in range(C):
                            last = nc.tensor.matmul(p_main[:, j // 2, (j % 2) * D + c * P:(j % 2) * D + (c + 1) * P],
                                                    IG[:, c, j * P:(j + 1) * P], centring[:, :], start=True, stop=True)
                    last.then_inc(mem_psum, 1)
                if stage == "og":
                    pe.wait_ge(og_ready, b + 1)
                    pe.wait_ge(gate_ready, 3 * C * (b + 1))
                    to_features(p_main, lambda j: HN[:, j, :], nj).then_inc(og_psum, 1)
                if stage == "wo":
                    if b == 0:
                        pe.wait_ge(w_lo, W_O)
                    pe.wait_ge(o_lo, C * (b + 1))
                    for j in range(nj):
                        cols = slice(j * P, (j + 1) * P)
                        for c in range(C):
                            last = mm3(p_main[:, j // 2, (j % 2) * D:(j % 2 + 1) * D], AH[:, c, cols], AL[:, c, cols],
                                       hi["wo"][:, c, :], lo["wo"][:, c, :], c == 0, c == C - 1)
                    last.then_inc(wo_psum, 1)
                if (stage, m) == ("h2", 0):
                    if b + 1 < NB:
                        pe.wait_ge(ht_ready, C * (b + 2))
                    to_features(p_main, lambda j: HN[:, j, :], nj, hn2_ready, old).then_inc(h2_psum, 1)
                if stage == "mup":
                    if m == 0:
                        pe.wait_ge(h2_lo, C * (b + 1))
                        if b == 0:
                            pe.wait_ge(w_lo, W_UP)
                    cols = slice(m * P, (m + 1) * P)
                    up_product(b, m, (H2H, H2L), P, lambda half, part, c: part[("wgt", "wvl")[half]][:, c, cols])
                if stage == "mdn":
                    if m == 0:
                        if b == 0:
                            pe.wait_ge(w_lo, W_OUT)
                        else:
                            pe.wait_ge(eacc_done, OUTPUTS * old)
                    mlp_down(b, m)
                if stage == "xt":
                    to_features(p_down, lambda j: HR[:, j, :], nj, xn_ready, old).then_inc(xt_psum, 1)
                if stage == "route":
                    pe.wait_ge(xt_lo, C * (b + 1))
                    if b == 0:
                        pe.wait_ge(wr_lo, 1)
                    for j in range(nj):
                        t = slice(j * P, (j + 1) * P)
                        for c in range(C):
                            last = mm3(p_route[:, j * RP:(j + 1) * RP], XTH[:, c, t], XTL[:, c, t], wrH[:, c, :], wrL[:, c, :],
                                       c == 0, c == C - 1)
                    last.then_inc(rt_psum, 1)
                if stage == "hid":
                    p, i = divmod(m, PK)
                    first, rows = CHUNK[i]
                    if i == 0:
                        pe.wait_ge(up_lo, b * PAIRS + p + 1)
                    if m == 0:
                        pe.wait_ge(xt_lo, C * (b + 1))
                    up_product(b, FM + m, (XTH, XTL), rows,
                               lambda half, part, c: part["up"][:, p % 2, c, half * PW + first:half * PW + first + rows])
                if stage == "dn":
                    expert_down(b, m)

            for name, b, m in steps("pe"):
                at(name, b, m)

        @block.vector
        def _(dve):
            n_dve = [0]

            def step(ins):
                n_dve[0] += 1
                ins.then_inc(s_dve, 1)

            def settle():
                dve.wait_ge(s_dve, n_dve[0])

            def link(ins):
                step(ins)
                settle()

            def guess(a, y):
                link(nc.vector.tensor_scalar(y.bitcast(I32), a.bitcast(I32), 1, None, ALU.logical_shift_right))
                step(nc.vector.tensor_scalar(y.bitcast(I32), y.bitcast(I32), -1.0, float(0x5F3759DF), ALU.mult, ALU.add))

            def newton(a, y, t, out):
                settle()
                link(nc.vector.tensor_tensor(t, y, y, ALU.mult))
                link(nc.vector.scalar_tensor_tensor(t, t, -0.5, a, ALU.mult, ALU.mult))
                return nc.vector.scalar_tensor_tensor(out, t, 1.5, y, ALU.add, ALU.mult)

            def rsqrt(out, a, y, t):
                guess(a, y)
                for i in range(2):
                    step(newton(a, y, t, y))
                return newton(a, y, t, out)

            def scratch(n):
                return va[:, 0:n], rs[:, 0:n], rt[:, 0:n]

            MINE, EXPERTS_OWN = (st, mv, va), (est, emv, eva)

            def stats(nj, tile, own):
                s, m, a = own
                for j in range(nj):
                    step(nc.vector.bn_stats(s[:, j, :], tile(j)))
                settle()
                for j in range(nj):
                    step(nc.vector.bn_aggr(m[:, j, :], s[:, j, :]))
                settle()
                link(nc.vector.tensor_scalar(a[:, 0:nj], m[:, 0:nj, 1], EPS, None, ALU.add))

            def minus_mean(nj, dst, scale, means):
                return nc.vector.scalar_tensor_tensor(dst[:, 0:nj], means[:, 0:nj, 0], -1.0, scale[:, 0:nj], ALU.mult, ALU.mult)

            step(nc.vector.memset(carry[:, :], 0.0))
            nc.vector.memset(HT[:, :, 0:KC - 1], 0.0).then_inc(halo_zero, 1)
            for e in range(E):
                step(nc.vector.memset(rank[:, e:e + 1], float(E - e)))
            settle()

            dve.wait_ge(ident_ready, 1)
            dve.wait_ge(same_head, 1)
            nc.vector.scalar_tensor_tensor(centring[:, :], centring[:, :], -1.0 / HD, ident[:, :], ALU.mult,
                                           ALU.add).then_inc(centring_ready, 1)

            def prepare_weights():
                dve.wait_ge(w_in["v"], 16)
                wv_raw = raw["qkv"][:, :, 2 * D:3 * D].rearrange("p c (h d) -> p c h d", d=HD)
                link(nc.vector.tensor_reduce(wmean[:, :, :], wv_raw, AX_X, ALU.add))
                link(nc.vector.tensor_scalar(wmean[:, :, :], wmean[:, :, :], -1.0 / HD, None, ALU.mult))
                nc.vector.tensor_tensor(wv_raw, wv_raw, wmean[:, :, :].unsqueeze(3).broadcast_to([P, C, HEADS, HD]),
                                        ALU.add).then_inc(w_centred, 1)
                dve.wait_ge(const_in, 64)
                nc.vector.tensor_copy(wgx[:, :, :].rearrange("p c (h d) -> p c h d", d=HD),
                                      wg16[:, :, :].unsqueeze(3).broadcast_to([P, C, HEADS, HD])).then_inc(wg_ready, 1)

            def flat(ap):
                return ap.rearrange("p j d -> p (j d)")

            def by_head(ap):
                return ap.rearrange("p (h d) -> p h d", d=HD)

            def spread(ap):
                return ap.unsqueeze(2).broadcast_to([P, ap.shape[1], HD])

            def wide(ap):
                return ap.unsqueeze(2).broadcast_to([P, ap.shape[1], E])

            def choose(nj, i):
                e8, ranks = ex[:, 0:nj, 0:E], rank[:, :].unsqueeze(1).broadcast_to([P, nj, E])
                src = e8 if i == 0 else key[:, 0:nj, :]
                link(nc.vector.tensor_reduce(top[:, 1, 0:nj], src, AX_X, ALU.max))
                link(nc.vector.tensor_tensor(pick[:, i, 0:nj], src, wide(top[:, 1, 0:nj]), ALU.is_equal))
                link(nc.vector.tensor_tensor(pick[:, i, 0:nj], pick[:, i, 0:nj], ranks, ALU.mult))
                link(nc.vector.tensor_reduce(top[:, 2, 0:nj], pick[:, i, 0:nj], AX_X, ALU.max))
                link(nc.vector.tensor_tensor(pick[:, i, 0:nj], pick[:, i, 0:nj], wide(top[:, 2, 0:nj]), ALU.is_equal))
                if i == 0:
                    step(nc.vector.scalar_tensor_tensor(key[:, 0:nj, :], pick[:, 0, 0:nj], -2.0, e8, ALU.mult, ALU.add))

            def weigh(nj):
                step(nc.vector.tensor_tensor(pick[:, 0, 0:nj], pick[:, 0, 0:nj], pick[:, 1, 0:nj], ALU.add))
                link(nc.vector.tensor_scalar(top[:, 2, 0:nj], ex[:, 0:nj, E], 1.0, None, ALU.add))
                step(nc.vector.reciprocal(cw[:, 0:nj, E], top[:, 2, 0:nj]))
                link(nc.vector.tensor_tensor(key[:, 0:nj, :], ex[:, 0:nj, 0:E], pick[:, 0, 0:nj], ALU.mult))
                link(nc.vector.tensor_reduce(top[:, 3, 0:nj], key[:, 0:nj, :], AX_X, ALU.add))
                link(nc.vector.reciprocal(top[:, 3, 0:nj], top[:, 3, 0:nj]))
                step(nc.vector.tensor_tensor(cw[:, 0:nj, 0:E], key[:, 0:nj, :], wide(top[:, 3, 0:nj]), ALU.mult))

            def at(stage, b, m):
                nj, old, new = TILES[b], START[b], START[b + 1]
                tb = nj * P
                xb = X[:, b % 2, 0:nj]
                m_flat = by_head(flat(HN[:, 0:nj, :]))
                G = nj * HEADS
                if stage == "ln0":
                    r, own = r0[:, b % 2, 0:nj], (hva[:, 0:nj], hrs[:, 0:nj], hrt[:, 0:nj])
                    if m == 0:
                        dve.wait_ge(h_in, 16 * (b + 1))
                        stats(nj, lambda j: QKV[:, j, 0:D], (hst, hmv, hva))
                    if m == 1:
                        link(rsqrt(r, *own))
                        step(minus_mean(nj, n0[:, b % 2], r0[:, b % 2], hmv))
                        link(nc.vector.tensor_tensor(own[0], hmv[:, 0:nj, 1], r, ALU.mult))
                        link(nc.vector.tensor_tensor(own[0], own[0], r, ALU.mult))
                        step(nc.vector.tensor_scalar(own[0], own[0], EPS, None, ALU.add))
                    if m == 2:
                        settle()
                        link(rsqrt(own[1], *own))
                        link(nc.vector.tensor_tensor(s1[:, 0:nj], r, own[1], ALU.mult))
                        minus_mean(nj, n1, s1, hmv).then_inc(ln0_ready, 1)
                        if b == 0:
                            prepare_weights()
                if stage == "conv":
                    if m == 0:
                        if b > 0:
                            dve.wait_ge(conv_lo, C * b)
                            dve.wait_ge(gate_psum, C * (3 * b - 1))
                        for c in range(C):
                            dve.wait_ge(ht_ready, C * b + c + 1)
                            step(nc.vector.tensor_scalar(XC[:, c, 0:tb], HT[:, c, 0:tb], v(c, CONVW), v(c, CONVB), ALU.mult,
                                                         ALU.add))
                    else:
                        settle()
                        for c in range(C):
                            ins = nc.vector.scalar_tensor_tensor(XC[:, c, 0:tb], HT[:, c, m:m + tb], v(c, CONVW + m),
                                                                 XC[:, c, 0:tb], ALU.mult, ALU.add)
                            if m < KC - 1:
                                step(ins)
                            else:
                                ins.then_inc(conv_done, 1)
                if stage == "q" and m < nj:
                    n = old + m
                    dve.wait_ge(sq_ready, n + 1)
                    if b > 0 and m == 0:
                        dve.wait_ge(g_ready, 2 * b)
                    nc.vector.tensor_reduce(rr[:, m, :], by_head(SQ[n % 2]), AX_X,
                                            ALU.add).then_inc(ss_done, 1)
                if stage == "rs":
                    a, y, t = scratch(nj * 3 * HEADS)
                    if m == 0:
                        dve.wait_ge(ss_done, new)
                        args = a.rearrange("p (j h) -> p j h", j=nj)
                        step(nc.vector.tensor_scalar(args[:, :, 0:2 * HEADS], rr[:, 0:nj, 0:2 * HEADS], 1e-12, None, ALU.add))
                        link(nc.vector.tensor_scalar(args[:, :, 2 * HEADS:], rr[:, 0:nj, 2 * HEADS:], 1.0 / HD, EPS,
                                                     ALU.mult, ALU.add))
                        guess(a, y)
                        step(newton(a, y, t, y))
                    else:
                        step(newton(a, y, t, y))
                        newton(a, y, t, rr[:, 0:nj, :].rearrange("p j h -> p (j h)")).then_inc(rr_ready, 1)
                if stage == "u":
                    k, w = heads(QKV[:, 0:nj, D:2 * D]), heads(QKV[:, 0:nj, 2 * D:3 * D])
                    settle()
                    if m == 0:
                        dve.wait_ge(rr_ready, b + 1)
                        dve.wait_ge(v_scaled, new)
                        step(nc.vector.tensor_tensor(w, w, per_head(rr[:, 0:nj, 2 * HEADS:]), ALU.mult))
                    if m == 1:
                        step(nc.vector.tensor_tensor(k, k, per_head(rr[:, 0:nj, HEADS:2 * HEADS]), ALU.mult))
                    if m == 2:
                        step(nc.vector.tensor_tensor(w, w, per_dim(nj, 1), ALU.add))
                    if m == 3:
                        nc.vector.tensor_tensor(w, w, k, ALU.mult).then_inc(u_ready, 1)
                if (stage, m) == ("scan", 0):
                    dve.wait_ge(gate_ready, C * (3 * b + 2))
                    dve.wait_ge(ut_psum, b + 1)
                    for c in range(C):
                        step(nc.vector.tensor_tensor(IG[:, c, 0:tb], IG[:, c, 0:tb], p_main[:, c, 0:tb], ALU.mult))
                if (stage, m) == ("scan", 1):
                    settle()
                    if b > 0:
                        dve.wait_ge(carry_kept, b)
                    for c in range(C):
                        nc.vector.tensor_tensor_scan(IG[:, c, 0:tb], GA[:, c, 0:tb], IG[:, c, 0:tb], carry[:, c:c + 1], ALU.mult,
                                                     ALU.add).then_inc(mem_ready, 1)
                    dve.wait_ge(mem_ready, C * (b + 1))
                    nc.vector.tensor_copy(carry[:, :], IG[:, :, tb - 1]).then_inc(carry_kept, 1)
                if stage == "mean":
                    settle()
                    link(nc.vector.tensor_reduce(mu[:, 0:G], m_flat, AX_X, ALU.add))
                    step(nc.vector.tensor_scalar(mu[:, 0:G], mu[:, 0:G], -1.0 / HD, None, ALU.mult))
                if stage == "centre":
                    settle()
                    nc.vector.tensor_tensor(m_flat, m_flat, spread(mu[:, 0:G]), ALU.add).then_inc(centred, 1)
                if stage == "var":
                    dve.wait_ge(msq_ready, 2 * b + m + 1)
                    link(nc.vector.tensor_reduce(va[:, 0:G], by_head(MSQ[:, 0:nj * D]), AX_X, ALU.add))
                    step(nc.vector.tensor_scalar(va[:, 0:G], va[:, 0:G], 1.0 / HD, EPS, ALU.mult, ALU.add))
                if stage == "rstd":
                    settle()
                    step(rsqrt(mu[:, 0:G], *scratch(G)))
                if stage == "norm":
                    settle()
                    if m == 0:
                        if b > 0:
                            dve.wait_ge(h2_psum, b)
                        nc.vector.tensor_tensor(m_flat, by_head(flat(p_main)[:, 0:nj * D]), spread(mu[:, 0:G]),
                                                ALU.mult).then_inc(normed, 1)
                    else:
                        nc.vector.tensor_tensor(m_flat, m_flat, spread(mu[:, 0:G]), ALU.mult).then_inc(og_ready, 1)
                if stage == "affine":
                    settle()
                    if m == 0:
                        dve.wait_ge(g_ready, 2 * (b + 1))
                        dve.wait_ge(normed, b + 1)
                        step(nc.vector.tensor_tensor(HN[:, 0:nj, :], HN[:, 0:nj, :], QKV[:, 0:nj, D:2 * D], ALU.mult))
                    else:
                        step(nc.vector.tensor_tensor(HN[:, 0:nj, :], HN[:, 0:nj, :], QKV[:, 0:nj, 2 * D:], ALU.add))
                if (stage, m) == ("o", 0):
                    for c in range(C):
                        dve.wait_ge(og_affine, C * b + c + 1)
                        dve.wait_ge(gate_ready, C * (3 * b + 2) + c + 1)
                        nc.vector.tensor_tensor(OG[:, c, 0:tb], OG[:, c, 0:tb], GA[:, c, 0:tb], ALU.mult).then_inc(o_ready, 1)
                if (stage, m) == ("o", 1):
                    for c in range(C):
                        dve.wait_ge(o_hi, C * b + c + 1)
                        nc.vector.tensor_tensor(AL[:, c, 0:tb], OG[:, c, 0:tb], f32(AH[:, c, 0:tb]), ALU.subtract).then_inc(o_lo, 1)
                if stage == "wo":
                    dve.wait_ge(wo_psum, b + 1)
                    dve.wait_ge(y0_ready, new)
                    if b > 0:
                        dve.wait_ge(xt_psum, b)
                    nc.vector.tensor_tensor(flat(HR[:, 0:nj, :]), flat(p_main)[:, 0:nj * D], flat(HN[:, 0:nj, :]), ALU.add).then_inc(hr_ready, 1)
                if (stage, m) == ("ln2", 0):
                    dve.wait_ge(hr_ready, b + 1)
                    stats(nj, lambda j: HR[:, j, :], MINE)
                if (stage, m) == ("ln2", 1):
                    link(rsqrt(l2r[:, 0:nj], *scratch(nj)))
                    minus_mean(nj, l2n, l2r, mv).then_inc(ln2_stats, 1)
                if (stage, m) == ("h2", 1):
                    for c in range(C):
                        dve.wait_ge(h2_hi, C * b + c + 1)
                        nc.vector.tensor_tensor(H2L[:, c, 0:tb], GA[:, c, 0:tb], f32(H2H[:, c, 0:tb]), ALU.subtract).then_inc(h2_lo, 1)
                if stage in ("mup", "hid"):
                    g, i, rows = hidden(stage, b, m)
                    dve.wait_ge(silu_ready, g + 1)
                    nc.vector.tensor_tensor(SM[0:rows, i, 0:tb], SM[0:rows, i, 0:tb], p_pair(g)[1][0:rows, 0:tb],
                                            ALU.mult).then_inc(hid_ready, 1)
                if (stage, m) == ("sum", 0):
                    dve.wait_ge(down_psum, downs(b, FM - 1))
                    dve.wait_ge(x_in[b % 2], 16 * (b // 2 + 1))
                    link(nc.vector.tensor_tensor(flat(HR[:, 0:nj, :]), flat(HR[:, 0:nj, :]), flat(p_down)[:, 0:nj * D], ALU.add))
                    stats(nj, lambda j: HR[:, j, :], EXPERTS_OWN)
                if (stage, m) == ("sum", 1):
                    link(rsqrt(ers[:, 0:nj], eva[:, 0:nj], ers[:, 0:nj], ert[:, 0:nj]))
                    for j in range(nj):
                        step(nc.vector.tensor_scalar(HR[:, j, :], HR[:, j, :], emv[:, j, 0:1], ers[:, j:j + 1],
                                                     ALU.subtract, ALU.mult))
                    settle()
                    step(nc.vector.tensor_tensor(xb, xb, HR[:, 0:nj, :], ALU.add))
                if (stage, m) == ("x2", 0):
                    settle()
                    stats(nj, lambda j: xb[:, j, :], EXPERTS_OWN)
                if (stage, m) == ("x2", 1):
                    link(rsqrt(x2r[:, 0:nj], eva[:, 0:nj], ers[:, 0:nj], ert[:, 0:nj]))
                    minus_mean(nj, x2n, x2r, emv).then_inc(x2_stats, 1)
                if stage == "xt":
                    for c in range(C):
                        dve.wait_ge(xt_hi, C * b + c + 1)
                        nc.vector.tensor_tensor(XTL[:, c, 0:tb], p_down[:, c, 0:tb], f32(XTH[:, c, 0:tb]), ALU.subtract).then_inc(xt_lo, 1)
                if stage == "route":
                    dve.wait_ge(rt_psum, b + 1)
                    nc.vector.tensor_copy(LG[:, 0:nj, :], p_route[:, 0:nj * RP].rearrange("p (j r) -> p j r", r=RP)[:, :, 0:RW]).then_inc(rt_copied, 1)
                if (stage, m) == ("choose", 0):
                    dve.wait_ge(rt_copied, b + 1)
                    step(nc.vector.tensor_reduce(top[:, 0, 0:nj], LG[:, 0:nj, 0:E], AX_X, ALU.max))
                    step(nc.vector.tensor_scalar(ex[:, 0:nj, E], LG[:, 0:nj, E], -1.0, None, ALU.mult))
                    settle()
                    nc.vector.tensor_tensor(ex[:, 0:nj, 0:E], LG[:, 0:nj, 0:E], wide(top[:, 0, 0:nj]), ALU.subtract).then_inc(lmax_ready, 1)
                if (stage, m) == ("choose", 1):
                    dve.wait_ge(exp_ready, b + 1)
                    choose(nj, 0)
                if (stage, m) == ("choose", 2):
                    settle()
                    choose(nj, 1)
                if (stage, m) == ("choose", 3):
                    weigh(nj)
                if stage == "dn" and (m // 2 < ROUTED or m % 2 == 1):
                    o = m if m // 2 < ROUTED else ROUTED + m // 2
                    e = min(o, E)
                    if m == 0:
                        settle()
                    for j in range(nj):
                        if j % 2 == 0:
                            dve.wait_ge(down_psum, downs(b, FM + m - 1) + j // 2 + 1)
                        part, weight = p_down[:, j // 2, (j % 2) * D:(j % 2 + 1) * D], cw[:, j, e:e + 1]
                        if o == 0:
                            nc.vector.tensor_scalar(acc[:, j, :], part, weight, None, ALU.mult).then_inc(eacc_done, 1)
                        else:
                            dve.wait_ge(eacc_done, OUTPUTS * old + (o - 1) * nj + j + 1)
                            nc.vector.scalar_tensor_tensor(acc[:, j, :], part, weight, acc[:, j, :], ALU.mult,
                                                           ALU.add).then_inc(eacc_done, 1)
                if (stage, m) == ("finish", 0):
                    dve.wait_ge(eacc_done, OUTPUTS * new)
                    stats(nj, lambda j: acc[:, j, :], EXPERTS_OWN)
                if (stage, m) == ("finish", 1):
                    link(rsqrt(ers[:, 0:nj], eva[:, 0:nj], ers[:, 0:nj], ert[:, 0:nj]))
                    for j in range(nj):
                        step(nc.vector.tensor_scalar(acc[:, j, :], acc[:, j, :], emv[:, j, 0:1], ers[:, j:j + 1],
                                                     ALU.subtract, ALU.mult))
                    settle()
                    for j in range(nj):
                        nc.vector.tensor_tensor(xb[:, j, :], xb[:, j, :], acc[:, j, :], ALU.add).then_inc(out_ready, 1)

            for name, b, m in steps("dve"):
                at(name, b, m)


def kernel(**inputs):
    import concourse.bacc as bacc
    from concourse.bass_utils import run_bass_kernel_spmd

    a = {k: np.ascontiguousarray(val) for k, val in inputs.items()}
    A, M = "L0_attn_", "L0_ffn_"

    def features(u):
        return np.reshape(u, (C, P, -1)).transpose(1, 0, 2)

    vecs = np.concatenate([features(a[A + n]) for n in ("ln1w", "ln1b")]
                          + [features(a[A + "conv_w"][:, 0, :])]
                          + [features(a[A + n]) for n in ("conv_b", "big", "bog")]
                          + [features(np.repeat(a[A + "bg"], HD))]
                          + [features(a[A + n]) for n in ("gnw", "gnb", "ln2w", "ln2b")], axis=2)
    headvecs = np.stack([a[A + n] for n in ("vnw", "vnb", "mnw", "mnb")])
    headvecs = np.broadcast_to(headvecs[None], (P, 4, HD))
    router = np.concatenate([a[M + "router_w"].T, a[M + "shared_gate_w"][:, None],
                             np.zeros((D, RP - RW), np.float32)], axis=1)
    def pairs(w, shared):
        both = w.reshape(ROUTED, 2, D, EI)
        routed = np.concatenate([both[:, 0, :, 0:P], both[:, 1, :, 0:P], both[:, 0, :, P:], both[:, 1, :, P:]], axis=2)
        return np.concatenate([routed, shared.reshape(D, PAIRS - ROUTED, PW).transpose(1, 0, 2)], axis=0)

    up = np.concatenate([pairs(a[M + "w_gate"], a[M + "sw_gate"]), pairs(a[M + "w_up"], a[M + "sw_up"])], axis=2)
    up = up.reshape(PAIRS, C, P, 2 * PW).transpose(0, 2, 1, 3)
    down = np.zeros((PAIRS, 4, P, D), np.float32)
    wd = a[M + "w_down"].reshape(ROUTED, 2, EI, D)
    down[:ROUTED, 0:2] = wd[:, :, 0:P]
    down[:ROUTED, 2, 0:EI - P] = wd[:, 0, P:]
    down[:ROUTED, 3, EI - P:LASTK] = wd[:, 1, P:]
    sd = a[M + "sw_down"].reshape(PAIRS - ROUTED, PW, D)
    down[ROUTED:, 0:2] = sd[:, 0:2 * P].reshape(PAIRS - ROUTED, 2, P, D)
    down[ROUTED:, 2, 0:LASTK] = sd[:, 2 * P:]
    down = down.transpose(0, 2, 1, 3)

    arrays = {
        "x": a[A + "x"].reshape(T, D), "wq": a[A + "Wq"], "wk": a[A + "Wk"], "wv": a[A + "Wv"],
        "wig": a[A + "Wig"], "wog": a[A + "Wog"], "wo": a[A + "Wo"], "wg": a[A + "Wg"],
        "wgate": a[A + "Wgate"], "wval": a[A + "Wval"], "wout": a[A + "Wout"],
        "vecs": vecs, "headvecs": headvecs, "router": features(router), "up": up, "down": down,
    }
    arrays = {k: np.ascontiguousarray(val) for k, val in arrays.items()}
    nc = bacc.Bacc("TRN2", target_bir_lowering=False, num_devices=1)
    args = [nc.dram_tensor(k, val.shape, mybir.dt.from_np(val.dtype), kind="ExternalInput").ap()
            for k, val in arrays.items()]
    args.append(nc.dram_tensor("out", (T, D), F32, kind="ExternalOutput").ap())
    build(nc, *args)
    r = run_bass_kernel_spmd(nc, [arrays], core_ids=[0])
    return r.results[0]["out"].reshape(1, T, D)
```
